# Optimizing a Trainium2 kernel written in Bass

```python
import numpy as np
import jax
import jax.numpy as jnp

def _softmax(x, axis=-1):
    return jax.nn.softmax(x, axis=axis)

def _gelu(x):
    return jax.nn.gelu(x, approximate=True)

def _silu(x):
    return jax.nn.silu(x)

def _sigmoid(x):
    return jax.nn.sigmoid(x)

def _layernorm(x, axis=-1, eps=1e-05):
    m = jnp.mean(x, axis=axis, keepdims=True)
    v = jnp.var(x, axis=axis, keepdims=True)
    return (x - m) / jnp.sqrt(v + eps)

def _scatter_add(tgt, idx, src, axis=0):
    return tgt.at[idx].add(src)

def _segment_sum(src, seg, n):
    return jax.ops.segment_sum(src, seg, n)
kernel_name = 'mk_early_fusion_d1_tok_img512_r4_20bc75'

def setup_inputs(seed: int=0):
    np.random.seed(seed)
    _w = jnp.asarray

    def _rec_inputs():
        import jax
        import jax.numpy as jnp
        _rk = jax.random.key(seed)
        x = -0.000147625 + 0.999875 * jax.random.normal(jax.random.fold_in(_rk, 1), (128, 3, 224, 224), jnp.float32)
        txt = 0.00355565 + 0.408319 * jax.random.normal(jax.random.fold_in(_rk, 2), (128, 77, 128), jnp.float32)
        return (x, txt)
    x, txt = _rec_inputs()

    def _L0_tok_setup():
        import jax, jax.numpy as jnp
        import numpy as np
        N_PATCHES = 8
        PATCH = 28
        C = 3
        IN_D = C * PATCH * PATCH
        HID = 128
        SEQ = N_PATCHES * N_PATCHES + 1

        def _positional_embedding(seq_len, dim):
            i = np.arange(seq_len)[:, None].astype(np.float32)
            j = np.arange(dim)[None, :].astype(np.float32)
            ang = i / np.power(100000.0, j / dim)
            pe = np.where(j % 2 == 0, np.sin(ang), np.cos(ang))
            return jnp.asarray(pe, dtype=jnp.float32)
        key = jax.random.key(seed)
        k1, k2, k3, k4 = jax.random.split(key, 4)
        B = 64
        X = jax.random.normal(k1, (B, C, 224, 224), dtype=jnp.float32)
        bound = 1.0 / np.sqrt(IN_D)
        W = jax.random.uniform(k2, (HID, IN_D), minval=-bound, maxval=bound, dtype=jnp.float32)
        b = jax.random.uniform(k3, (HID,), minval=-bound, maxval=bound, dtype=jnp.float32)
        class_token = jax.random.uniform(k4, (1, HID), dtype=jnp.float32)
        pos_embed = _positional_embedding(SEQ, HID)
        return {'X': X, 'W': W, 'b': b, 'class_token': class_token, 'pos_embed': pos_embed}
    _L0_tok_all = _L0_tok_setup()
    _L0_tok_in = {k: v for k, v in _L0_tok_all.items() if k in ('W', 'b', 'class_token', 'pos_embed')}
    del _L0_tok_all

    def _L0_attn_setup():
        import jax, jax.numpy as jnp
        import numpy as np
        B, N, DIM, DD = (32, 1024, 128, 128)
        SCALE = DD ** (-0.5)
        key = jax.random.key(seed)
        ks = jax.random.split(key, 7)
        return {'x': jax.random.normal(ks[0], (B, N, DIM), dtype=jnp.float32), 'Wq': jax.random.normal(ks[1], (DIM, DD), dtype=jnp.float32) * DIM ** (-0.5), 'Wk': jax.random.normal(ks[2], (DIM, DD), dtype=jnp.float32) * DIM ** (-0.5), 'Wv': jax.random.normal(ks[3], (DIM, DD), dtype=jnp.float32) * DIM ** (-0.5), 'Wr': jax.random.normal(ks[4], (DD, DD), dtype=jnp.float32) * DD ** (-0.5), 'alpha': jax.random.normal(ks[5], (DD,), dtype=jnp.float32), 'beta': jax.random.normal(ks[6], (DD,), dtype=jnp.float32)}
    _L0_attn_all = _L0_attn_setup()
    _L0_attn_in = {k: v for k, v in _L0_attn_all.items() if k in ('Wq', 'Wk', 'Wv', 'Wr', 'alpha', 'beta')}
    del _L0_attn_all

    def _L0_ffn_setup():
        import jax, jax.numpy as jnp
        import numpy as np
        import math
        D_MODEL = 128
        N_EXPERTS = 128
        TOP_K = 8
        N_HEADS = 8
        D_KEYS = 128
        HALF = D_KEYS // 2
        N_BATCH, T_SEQ = (2, 512)
        key = jax.random.key(seed)
        k1, k2, k3, k4, k5, k6 = jax.random.split(key, 6)
        queries = jax.random.normal(k1, (N_BATCH, T_SEQ, D_MODEL), dtype=jnp.float32)
        bound_q = 1.0 / math.sqrt(D_MODEL)
        Wq = jax.random.uniform(k2, (N_HEADS * D_KEYS, D_MODEL), minval=-bound_q, maxval=bound_q, dtype=jnp.float32)
        bq = jax.random.uniform(k3, (N_HEADS * D_KEYS,), minval=-bound_q, maxval=bound_q, dtype=jnp.float32)
        bound_k = 1.0 / math.sqrt(HALF)
        keys = jax.random.uniform(k4, (N_HEADS, 2, N_EXPERTS, HALF), minval=-bound_k, maxval=bound_k, dtype=jnp.float32)
        std = D_MODEL ** (-0.5)
        w_down_embed = std * jax.random.normal(k5, (N_EXPERTS * N_EXPERTS, D_MODEL), dtype=jnp.float32)
        w_up_embed = std * jax.random.normal(k6, (N_EXPERTS * N_EXPERTS, D_MODEL), dtype=jnp.float32)
        return {'queries': queries, 'Wq': Wq, 'bq': bq, 'keys': keys, 'w_down_embed': w_down_embed, 'w_up_embed': w_up_embed}
    _L0_ffn_all = _L0_ffn_setup()
    _L0_ffn_in = {k: v for k, v in _L0_ffn_all.items() if k in ('Wq', 'bq', 'keys', 'w_down_embed', 'w_up_embed')}
    del _L0_ffn_all
    return {'x': x, 'txt': txt, 'L0_tok_W': _L0_tok_in['W'], 'L0_tok_b': _L0_tok_in['b'], 'L0_tok_class_token': _L0_tok_in['class_token'], 'L0_tok_pos_embed': _L0_tok_in['pos_embed'], 'L0_attn_Wq': _L0_attn_in['Wq'], 'L0_attn_Wk': _L0_attn_in['Wk'], 'L0_attn_Wv': _L0_attn_in['Wv'], 'L0_attn_Wr': _L0_attn_in['Wr'], 'L0_attn_alpha': _L0_attn_in['alpha'], 'L0_attn_beta': _L0_attn_in['beta'], 'L0_ffn_Wq': _L0_ffn_in['Wq'], 'L0_ffn_bq': _L0_ffn_in['bq'], 'L0_ffn_keys': _L0_ffn_in['keys'], 'L0_ffn_w_down_embed': _L0_ffn_in['w_down_embed'], 'L0_ffn_w_up_embed': _L0_ffn_in['w_up_embed']}

def reference(x, txt, L0_tok_W, L0_tok_b, L0_tok_class_token, L0_tok_pos_embed, L0_attn_Wq, L0_attn_Wk, L0_attn_Wv, L0_attn_Wr, L0_attn_alpha, L0_attn_beta, L0_ffn_Wq, L0_ffn_bq, L0_ffn_keys, L0_ffn_w_down_embed, L0_ffn_w_up_embed):
    import jax
    import jax.numpy as jnp

    def _L0_tok_ref(X, W, b, class_token, pos_embed):
        import jax, jax.numpy as jnp
        import numpy as np
        N_PATCHES = 8
        PATCH = 28
        C = 3
        IN_D = C * PATCH * PATCH
        HID = 128
        SEQ = N_PATCHES * N_PATCHES + 1

        def _positional_embedding(seq_len, dim):
            i = np.arange(seq_len)[:, None].astype(np.float32)
            j = np.arange(dim)[None, :].astype(np.float32)
            ang = i / np.power(100000.0, j / dim)
            pe = np.where(j % 2 == 0, np.sin(ang), np.cos(ang))
            return jnp.asarray(pe, dtype=jnp.float32)
        B = X.shape[0]
        patches = X.reshape(B, C, N_PATCHES, PATCH, N_PATCHES, PATCH)
        patches = patches.transpose(0, 2, 4, 1, 3, 5).reshape(B, N_PATCHES * N_PATCHES, IN_D)
        tokens = jnp.einsum('bpi,hi->bph', patches, W) + b
        cls = jnp.broadcast_to(class_token[None, :, :], (B, 1, HID))
        tokens = jnp.concatenate([cls, tokens], axis=1)
        return tokens * pos_embed[None, :, :]

    def _L0_attn_ref(x, Wq, Wk, Wv, Wr, alpha, beta):
        import jax, jax.numpy as jnp
        import numpy as np
        B, N, DIM, DD = (32, 1024, 128, 128)
        SCALE = DD ** (-0.5)
        q = jnp.einsum('bni,id->bnd', x, Wq)
        k = jnp.einsum('bni,id->bnd', x, Wk)
        v = jnp.einsum('bni,id->bnd', x, Wv)
        alpha_w = jax.nn.softmax(q * alpha * SCALE, axis=-1)
        global_query = jnp.sum(q * alpha_w, axis=1)
        p = global_query[:, None, :] * k
        beta_w = jax.nn.softmax(p * beta * SCALE, axis=-1)
        global_key = jnp.sum(p * beta_w, axis=1)
        kv = global_key[:, None, :] * v
        out = jnp.einsum('bnd,de->bne', kv, Wr) + q
        return out

    def _L0_ffn_ref(queries, Wq, bq, keys, w_down_embed, w_up_embed):
        import jax, jax.numpy as jnp
        import numpy as np
        import math
        D_MODEL = 128
        N_EXPERTS = 128
        TOP_K = 8
        N_HEADS = 8
        D_KEYS = 128
        HALF = D_KEYS // 2
        N_BATCH, T_SEQ = (2, 512)
        N, T, D = queries.shape
        H, E, K = (N_HEADS, N_EXPERTS, TOP_K)
        q_tok = queries.reshape(-1, D)
        qh = q_tok @ Wq.T + bq
        qh = qh.reshape(-1, H, 2, HALF)
        sub_scores = jnp.einsum('nhcf,hcef->nhce', qh, keys)
        s, idx = jax.lax.top_k(sub_scores, K)
        all_scores = (s[:, :, 0, :, None] + s[:, :, 1, None, :]).reshape(-1, H, K * K)
        all_idx = (idx[:, :, 0, :, None] * E + idx[:, :, 1, None, :]).reshape(-1, H, K * K)
        best_s, best_pos = jax.lax.top_k(all_scores, K)
        indices = jnp.take_along_axis(all_idx, best_pos, axis=-1)
        w_down = w_down_embed[indices]
        w_up = w_up_embed[indices]
        x = jnp.einsum('nd,nhkd->nhk', q_tok, w_down)
        x = jax.nn.gelu(x)
        vals = x * jax.nn.softmax(best_s, axis=-1)
        out = jnp.einsum('nhk,nhkd->nd', vals, w_up)
        return out.reshape(N, T, D)
    h = _L0_tok_ref(x, L0_tok_W, L0_tok_b, L0_tok_class_token, L0_tok_pos_embed)
    h = jnp.concatenate([h, txt], axis=1)
    h = h + _L0_attn_ref(_layernorm(h, axis=-1), L0_attn_Wq, L0_attn_Wk, L0_attn_Wv, L0_attn_Wr, L0_attn_alpha, L0_attn_beta)
    h = h + _L0_ffn_ref(_layernorm(h, axis=-1), L0_ffn_Wq, L0_ffn_bq, L0_ffn_keys, L0_ffn_w_down_embed, L0_ffn_w_up_embed)
    return h

_drawn_inputs = setup_inputs


def setup_inputs(seed=0):
    import zlib

    import numpy as np

    out = dict(_drawn_inputs(seed))
    spreads = {}
    factors = {'L0_tok_b': 3.543,
     'L0_attn_Wk': 3.596,
     'L0_attn_Wv': 3.452,
     'L0_attn_Wr': 3.474,
     'L0_attn_alpha': 4.174,
     'L0_attn_beta': 7.552,
     'L0_ffn_Wq': 38.018,
     'L0_ffn_bq': 64.0,
     'L0_ffn_keys': 43.544,
     'L0_ffn_w_down_embed': 42.135,
     'L0_ffn_w_up_embed': 43.222}
    for name, (base, spread) in spreads.items():
        noise = np.random.default_rng([zlib.crc32(name.encode()), seed]).standard_normal(out[name].shape)
        drawn = base * np.exp(spread * noise) if base else spread * noise
        out[name] = jnp.asarray(drawn.astype(out[name].dtype))
    for name, factor in factors.items():
        out[name] = (out[name] * factor).astype(out[name].dtype)
    return out
```

```python
from contextlib import ExitStack

import concourse.bass as bass
from concourse import mybir

F32 = mybir.dt.float32
U32 = mybir.dt.uint32
ALU = mybir.AluOpType
ACT = mybir.ActivationFunctionType
AX = mybir.AxisListType

P = 128
D = 128
GRID, PATCH, CH = 8, 28, 3
IMG = GRID * PATCH
N_PATCH = GRID * GRID
N_TXT = 77
N_IMG_TOK = N_PATCH + 1
N_POS = N_IMG_TOK + N_TXT
EPS = 1e-5
SCALE = float(D) ** -0.5

ROWS = 4
KC = ROWS * PATCH
STRIPS = PATCH // ROWS
CHUNKS = CH * STRIPS
X_RING = 3
T_RING = 3
HALF = GRID // 2

GRP = 4
N_GRP = -(-N_POS // GRP)
BUFS = 2
BANK = 512

HEADS, TOPK, EXP = 8, 8, 128
PAIRS = [(0, 1, 8), (1, 1, 4), (2, 2, 2), (4, 4, 1)]
N_CAND = sum(ni * nj for _, ni, nj in PAIRS)
ROW = 2 * D
GELU_C = 0.7978845608028654
GELU_K = 0.044715


def group_size(g):
    return N_POS - GRP * g if isinstance(g, int) and g == N_GRP - 1 else GRP


def run_skewed(eng, count, stages):
    deepest = max(lag for lag, _ in stages)

    def step(s, parity_of_step, pair):
        for lag, fn in stages:
            if isinstance(s, int):
                if 0 <= s - lag < count:
                    fn(s - lag, (s - lag) % BUFS, (s - lag) // BUFS)
            else:
                parity = (parity_of_step - lag) % BUFS
                fn(s - lag, parity, pair - (lag + parity - parity_of_step) // BUFS)

    first = -(-deepest // BUFS) * BUFS
    last = first + (count - 1 - first) // BUFS * BUFS
    for s in range(first):
        step(s, None, None)
    with eng.Fori(first // BUFS, last // BUFS) as pair:
        for u in range(BUFS):
            step(pair * BUFS + u, u, pair)
    for s in range(last, count + deepest):
        step(s, None, None)


class Core:
    pass


def wait_at_gate(eng, sem, value, gate):
    eng.wait_ge(sem, value)
    eng.sem_inc(gate, 1)


def new_semaphores(nc, ctx, prefix, names):
    return [ctx.enter_context(nc.semaphore(f"{prefix}_{n}")) for n in names.split()]


def blocks_of(ap, n, width=D):
    return ap.rearrange("p (n d) -> p n d", d=width)


def bcast_mid(ap, n):
    return ap.unsqueeze(1).to_broadcast([ap.shape[0], n, ap.shape[1]])


def bcast_last(ap, n):
    return ap.unsqueeze(2).to_broadcast([ap.shape[0], ap.shape[1], n])


def build_embed(nc, m, x, txt, tok_wT, tok_b, cls, pos, attn_w, alpha, beta, wqT, bq, keysT):
    with ExitStack() as ctx:
        (sorted_, const_in, weights_in, zeroed, ident_made, transposed, dve_copied, act_copied,
         chunk_done, acc_read, cls_made) = new_semaphores(
            nc, ctx, "e", "sorted const_in weights_in zeroed ident_made transposed "
            "dve_copied act_copied chunk_done acc_read cls_made")
        X_CREDIT = 2 * X_RING
        x_in = [ctx.enter_context(nc.semaphore(f"e_x_in{i}")) for i in range(X_RING)]

        o = 0
        xbuf = m.work[:, o:o + X_RING * ROWS * IMG].rearrange("p (s r w) -> p s r w", s=X_RING, w=IMG)
        o += X_RING * ROWS * IMG
        xsort = m.work[:, o:o + X_RING * ROWS * IMG].rearrange("p (s g k) -> p s g k", s=X_RING, g=GRID)
        o += X_RING * ROWS * IMG
        xT = m.work[:, o:o + T_RING * GRID * P].rearrange("p (s g b) -> p s g b", s=T_RING, b=P)
        o += T_RING * GRID * P
        posb = m.work[:, o:o + N_IMG_TOK * D].rearrange("p (n d) -> p n d", d=D)
        wT = m.scratch[0:KC, 0:CHUNKS * D].rearrange("p (k d) -> p k d", d=D)
        o = CHUNKS * D
        ones = m.scratch[0:1, o:o + P]
        bias4 = m.scratch[0:1, o + P:o + P + BANK]
        clsb = m.scratch[:, o + P + BANK:o + P + BANK + D]
        acc = m.ps[:, 0:2, :]
        tp = m.ps[0:KC, 2:2 + 2 * T_RING, :]
        x_v = x.rearrange("b c (g s r) w -> b c g s (r w)", g=GRID, r=ROWS)
        N_CONST = 5

        block = ctx.enter_context(nc.Block())

        @block.sync
        def _(sp):
            sp.dma_start(wT, tok_wT).then_inc(const_in, 16)
            sp.dma_start(posb, pos.rearrange("n d -> (n d)").partition_broadcast(P)
                         .rearrange("p (n d) -> p n d", d=D)).then_inc(const_in, 16)
            for r in range(4):
                sp.dma_start(bias4[:, r * D:(r + 1) * D], tok_b.rearrange("(a d) -> a d", a=1)).then_inc(const_in, 16)
            sp.dma_start(clsb, cls.rearrange("a d -> (a d)").partition_broadcast(P)).then_inc(const_in, 16)
            with sp.Fori(0, GRID) as gy:
                for k in range(CHUNKS):
                    sp.wait_ge(sorted_, gy * CHUNKS + (k + 1))
                    sp.dma_start(xbuf[:, k % X_RING].rearrange("p r w -> p (r w)"),
                                 x_v[:, k // STRIPS, gy, k % STRIPS, :]).then_inc(x_in[k % X_RING], 16)

        @block.scalar
        def _(act):
            act.dma_start(m.h[:, N_IMG_TOK:N_POS, :], txt).then_inc(weights_in, 16)
            for n, w in enumerate(attn_w):
                act.dma_start(m.attn_w[:, n, :], w).then_inc(weights_in, 16)
            act.dma_start(m.alphab[:, :], alpha.partition_broadcast(P)).then_inc(weights_in, 16)
            act.dma_start(m.betab[:, :], beta.partition_broadcast(P)).then_inc(weights_in, 16)
            act.dma_start(m.wqT[:, :], wqT).then_inc(weights_in, 16)
            act.dma_start(m.bq[:, :], bq).then_inc(weights_in, 16)
            act.wait_ge(zeroed, 1)
            for half in range(2):
                act.dma_start(m.keys[64 * half:64 * half + 64, :, EXP * half:EXP * half + EXP],
                              keysT[64 * half:64 * half + 64]).then_inc(weights_in, 16)
            act.sem_inc(act_copied, T_RING)
            with act.Fori(0, GRID) as gy:
                for k in range(CHUNKS):
                    n = gy * CHUNKS + k
                    act.wait_ge(transposed, n * 2 + (X_CREDIT + 2))
                    act.wait_ge(chunk_done, n + 1)
                    nc.scalar.activation(xT[0:KC, k % T_RING, HALF:GRID, :],
                                         blocks_of(tp[:, 2 * (k % T_RING) + 1, :], HALF), ACT.Copy).then_inc(act_copied, 1)
            act.wait_ge(weights_in, 16 * (5 + len(attn_w) + 2))

        @block.gpsimd
        def _(pool):
            pool.memset(m.keys[:, :, :], 0.0).then_inc(zeroed, 1)
            pool.memset(m.ident[:, :], 0.0).then_inc(zeroed, 1)
            pool.wait_ge(zeroed, 2)
            pool.affine_select(out=m.ident[:, :], in_=m.ident[:, :], compare_op=ALU.not_equal, fill=1.0,
                               base=0, pattern=[[-1, P]], channel_multiplier=1).then_inc(ident_made, 1)
            pool.memset(ones, 1.0).then_inc(ident_made, 1)
            pool.iota(m.cand_no[:, :], pattern=[[1, N_CAND]], base=0, channel_multiplier=0,
                      allow_small_or_imprecise_dtypes=True)

        @block.tensor
        def _(pe):
            pe.sem_inc(transposed, X_CREDIT)
            pe.sem_inc(chunk_done, T_RING)
            pe.wait_ge(ident_made, 2)
            pe.wait_ge(const_in, 16 * (N_CONST + 2))

            def transposes(gy, k, half):
                n = gy * CHUNKS + k
                pe.wait_ge([dve_copied, act_copied][half], n + 1)
                for g in range(HALF):
                    gx = HALF * half + g
                    last = pe.transpose(tp[:, 2 * (k % T_RING) + half, g * P:(g + 1) * P],
                                        xsort[:, k % X_RING, gx, :], m.ident[:, :])
                last.then_inc(transposed, 1)

            def products(gy, k):
                n = gy * CHUNKS + k
                pe.wait_ge(dve_copied, n + 1 + T_RING)
                pe.wait_ge(act_copied, n + 1 + T_RING)
                for g in range(GRID):
                    last = pe.matmul(acc[:, g // HALF, (g % HALF) * D:(g % HALF + 1) * D],
                                     xT[0:KC, k % T_RING, g, :], wT[:, k, :], start=False,
                                     stop=(k == CHUNKS - 1 and g % HALF == HALF - 1), skip_group_check=True)
                last.then_inc(chunk_done, 1)

            with pe.Fori(0, GRID) as gy:
                pe.wait_ge(acc_read, gy + 1)
                for b in range(2):
                    pe.matmul(acc[:, b, :], ones, bias4, start=True, stop=False, skip_group_check=True)
                for k in range(CHUNKS):
                    pe.wait_ge(sorted_, gy * CHUNKS + (k + 1 + X_RING))
                    transposes(gy, k, 0)
                    transposes(gy, k, 1)
                    if k:
                        products(gy, k - 1)
                products(gy, CHUNKS - 1)

        @block.vector
        def _(dve):
            dve.sem_inc(sorted_, X_RING)
            dve.sem_inc(dve_copied, T_RING)
            dve.sem_inc(acc_read, 1)
            dve.wait_ge(const_in, 16 * (N_CONST + 2))
            dve.tensor_tensor(m.h[:, 0, :], clsb, posb[:, 0, :], ALU.mult).then_inc(cls_made, 1)
            with dve.Fori(0, GRID) as gy:
                for k in range(CHUNKS):
                    n = gy * CHUNKS + k
                    dve.wait_ge(x_in[k % X_RING], (gy * (CHUNKS // X_RING) + (k // X_RING + 1)) * 16)
                    dve.wait_ge(transposed, n * 2 + 2)
                    dve.tensor_copy(xsort[:, k % X_RING].rearrange("p g (r w) -> p g r w", w=PATCH),
                                    xbuf[:, k % X_RING].rearrange("p r (g w) -> p g r w", w=PATCH)).then_inc(sorted_, 1)
                    dve.wait_ge(transposed, n * 2 + (X_CREDIT + 1))
                    dve.wait_ge(chunk_done, n + 1)
                    dve.tensor_copy(xT[0:KC, k % T_RING, 0:HALF, :],
                                    blocks_of(tp[:, 2 * (k % T_RING), :], HALF)).then_inc(dve_copied, 1)
                dve.wait_ge(chunk_done, gy * CHUNKS + CHUNKS + T_RING)
                for b in range(2):
                    at = gy * GRID + (1 + HALF * b)
                    last = dve.tensor_tensor(m.h[:, bass.ds(at, HALF), :], blocks_of(acc[:, b, :], HALF),
                                             posb[:, bass.ds(at, HALF), :], ALU.mult)
                last.then_inc(acc_read, 1)


def reciprocal_deviations(nc, dve, act, m, step, root_done, variances_ready):
    var, t = m.stat[:, :, 1], m.newton
    if act is not None:
        act.wait_ge(step, variances_ready + 1)
        nc.scalar.activation(m.rstd[:, :], t[:, :], ACT.Sqrt).then_inc(root_done, 1)
        return
    dve.wait_ge(step, variances_ready)
    dve.tensor_scalar(t[:, :], var, EPS, None, ALU.add).then_inc(step, 1)
    dve.wait_ge(root_done, 1)
    dve.reciprocal(m.rstd[:, :], m.rstd[:, :]).then_inc(step, 1)
    dve.wait_ge(step, variances_ready + 2)
    dve.tensor_tensor(t[:, :], t[:, :], m.rstd[:, :], ALU.mult).then_inc(step, 1)
    dve.wait_ge(step, variances_ready + 3)
    dve.tensor_tensor(t[:, :], t[:, :], m.rstd[:, :], ALU.mult).then_inc(step, 1)
    dve.wait_ge(step, variances_ready + 4)
    dve.tensor_scalar(t[:, :], t[:, :], -0.5, 1.5, ALU.mult, ALU.add).then_inc(step, 1)
    dve.wait_ge(step, variances_ready + 5)
    dve.tensor_tensor(m.rstd[:, :], m.rstd[:, :], t[:, :], ALU.mult).then_inc(step, 1)
    dve.wait_ge(step, variances_ready + 6)


def group_statistics(dve, m, at, n, step, before, gate):
    dve.sem_inc(gate, 1)
    for j in range(n):
        last = dve.bn_stats(m.bn6[:, j, :], m.h[:, at + j, :])
    last.then_inc(step, 1)
    wait_at_gate(dve, step, before + 1, gate)
    for j in range(n):
        last = dve.bn_aggr(m.bn2[:, j, :], m.bn6[:, j, :])
    last.then_inc(step, 1)
    dve.wait_ge(step, before + 2)
    dve.tensor_copy(m.stat[:, bass.ds(at, n), :], m.bn2[:, 0:n, :]).then_inc(step, 1)


def build_statistics(nc, m):
    with ExitStack() as ctx:
        step, root_done, gate = new_semaphores(nc, ctx, "n", "step root_done gate")
        block = ctx.enter_context(nc.Block())

        @block.vector
        def _(dve):
            dve.tensor_scalar(m.alphab[:, :], m.alphab[:, :], SCALE, None, ALU.mult)
            dve.tensor_scalar(m.betab[:, :], m.betab[:, :], SCALE, None, ALU.mult)
            with dve.Fori(0, N_GRP - 1) as g:
                group_statistics(dve, m, g * GRP, GRP, step, g * 3, gate)
            group_statistics(dve, m, (N_GRP - 1) * GRP, group_size(N_GRP - 1), step, 3 * (N_GRP - 1), gate)
            reciprocal_deviations(nc, dve, None, m, step, root_done, 3 * N_GRP)

        @block.scalar
        def _(act):
            reciprocal_deviations(nc, None, act, m, step, root_done, 3 * N_GRP)


class Softmax:

    def __init__(self, m):
        o = 0

        def take(n):
            nonlocal o
            o += n
            return m.scratch[:, o - n:o]

        self.xn = [take(BANK) for _ in range(BUFS)]
        self.xT = [take(BANK) for _ in range(BUFS)]
        self.s = [take(BANK) for _ in range(BUFS)]
        self.e = [take(BANK) for _ in range(BUFS)]
        self.r = [take(BANK) for _ in range(BUFS)]
        self.w = [take(BANK) for _ in range(BUFS)]
        self.neg_max = [take(GRP) for _ in range(BUFS)]
        self.sum = [take(GRP) for _ in range(BUFS)]
        self.rec = [take(GRP) for _ in range(BUFS)]
        assert o <= SCRATCH


def softmax_stages(nc, m, b, sems, r_bank, total):
    (logits, exped, weighed, divided, summed) = sems

    def exps(act):
        def fn(g, p, pair):
            act.wait_ge(logits, g + 1 + BUFS)
            act.wait_ge(weighed, g + 1)
            for j in range(group_size(g)):
                last = nc.scalar.activation(b.e[p][:, j * D:(j + 1) * D], b.s[p][:, j * D:(j + 1) * D], ACT.Exp,
                                            bias=b.neg_max[p][:, j:j + 1], accum_out=b.sum[p][:, j:j + 1])
            last.then_inc(exped, 1)
        return fn

    def divide(pool):
        def fn(g, p, pair):
            n = group_size(g)
            pool.wait_ge(weighed, g + 1 + BUFS)
            w = blocks_of(b.w[p][:, 0:n * D], n)
            pool.tensor_tensor(w, w, bcast_last(b.rec[p][:, 0:n], D), ALU.mult).then_inc(divided, 1)
        return fn

    def sum_up(pe):
        def fn(g, p, pair):
            n = group_size(g)
            pe.wait_ge(divided, g + 1)
            pe.matmul(total[:, 0:n * D], m.ident[:, :], b.w[p][:, 0:n * D], start=isinstance(g, int) and g == 0,
                      stop=isinstance(g, int) and g == N_GRP - 1, skip_group_check=True).then_inc(summed, 1)
        return fn

    return exps, divide, sum_up


def build_query(nc, m):
    b = Softmax(m)
    with ExitStack() as ctx:
        (normed, norm_step, turned, copied, projected, logits, exped, weighed, divided, summed,
         step, done) = new_semaphores(nc, ctx, "q", "normed norm_step turned copied projected logits "
                                      "exped weighed divided summed step done")
        saved = [ctx.enter_context(nc.semaphore(f"q_saved{p}")) for p in range(BUFS)]
        turn = [m.ps[:, p, :] for p in range(BUFS)]
        q = [m.ps[:, 2 + p, :] for p in range(BUFS)]
        total = m.ps[:, 4, :]
        exps, divide, sum_up = softmax_stages(nc, m, b, (logits, exped, weighed, divided, summed), q, total)
        block = ctx.enter_context(nc.Block())

        @block.gpsimd
        def _(pool):
            def norm(g, p, pair):
                n, at = group_size(g), g * GRP
                x = blocks_of(b.xn[p][:, 0:n * D], n)
                pool.wait_ge(turned, g + 1)
                pool.tensor_tensor(x, m.h[:, bass.ds(at, n), :],
                                   m.stat[:, bass.ds(at, n), 0:1].to_broadcast([P, n, D]), ALU.subtract).then_inc(norm_step, 1)
                pool.wait_ge(norm_step, g + 1)
                pool.tensor_tensor(x, x, m.rstd[:, bass.ds(at, n)].unsqueeze(2).to_broadcast([P, n, D]),
                                   ALU.mult).then_inc(normed, 1)

            run_skewed(pool, N_GRP, [(0, norm), (2, divide(pool))])

        @block.sync
        def _(sp):
            for p in range(BUFS):
                sp.sem_inc(saved[p], 16)

            def save(g, p, pair):
                n, at = group_size(g), g * GRP
                sp.wait_ge(copied, g + 1 + BUFS)
                sp.dma_start(m.work[:, bass.ds(at * D, n * D)], b.xT[p][:, 0:n * D]).then_inc(saved[p], 16)

            run_skewed(sp, N_GRP, [(0, save)])
            for p in range(BUFS):
                sp.wait_ge(saved[p], 16 * (1 + N_GRP // BUFS))

        @block.scalar
        def _(act):
            act.sem_inc(copied, BUFS)
            act.sem_inc(exped, BUFS)

            def copy(g, p, pair):
                n = group_size(g)
                act.wait_ge(turned, g + 1 + BUFS)
                act.wait_ge(projected, g + 1)
                act.wait_ge(saved[p], pair * 16 + 16)
                nc.scalar.activation(b.xT[p][:, 0:n * D], turn[p][:, 0:n * D], ACT.Copy).then_inc(copied, 1)

            run_skewed(act, N_GRP, [(0, copy), (1, exps(act))])

        @block.tensor
        def _(pe):
            pe.sem_inc(turned, BUFS)
            pe.sem_inc(projected, BUFS)
            pe.sem_inc(summed, BUFS)

            def turn_over(g, p, pair):
                pe.wait_ge(normed, g + 1)
                pe.wait_ge(copied, g + 1)
                for j in range(group_size(g)):
                    last = pe.transpose(turn[p][:, j * D:(j + 1) * D], b.xn[p][:, j * D:(j + 1) * D], m.ident[:, :])
                last.then_inc(turned, 1)

            def project(g, p, pair):
                pe.wait_ge(copied, g + 1 + BUFS)
                pe.wait_ge(weighed, g + 1)
                for j in range(group_size(g)):
                    last = pe.matmul(q[p][:, j * D:(j + 1) * D], b.xT[p][:, j * D:(j + 1) * D], m.attn_w[:, 0, :],
                                     start=True, stop=True)
                last.then_inc(projected, 1)

            run_skewed(pe, N_GRP, [(0, turn_over), (1, project), (3, sum_up(pe))])

        @block.vector
        def _(dve):
            dve.sem_inc(logits, BUFS)
            dve.sem_inc(weighed, BUFS)

            def logit(g, p, pair):
                n = group_size(g)
                s = blocks_of(b.s[p][:, 0:n * D], n)
                dve.wait_ge(projected, g + 1 + BUFS)
                dve.wait_ge(exped, g + 1)
                dve.tensor_tensor(s, blocks_of(q[p][:, 0:n * D], n), bcast_mid(m.alphab[:, :], n), ALU.mult).then_inc(step, 1)
                dve.wait_ge(step, g + 1)
                dve.tensor_reduce(b.neg_max[p][:, 0:n], s, AX.X, ALU.max, negate=True).then_inc(logits, 1)

            def weigh(g, p, pair):
                n = group_size(g)
                hg = m.h[:, bass.ds(g * GRP, n), :]
                q_g = blocks_of(q[p][:, 0:n * D], n)
                dve.wait_ge(exped, g + 1 + BUFS)
                dve.wait_ge(summed, g + 1)
                dve.reciprocal(b.rec[p][:, 0:n], b.sum[p][:, 0:n])
                dve.tensor_tensor(hg, hg, q_g, ALU.add)
                dve.tensor_tensor(b.w[p][:, 0:n * D], b.e[p][:, 0:n * D], q[p][:, 0:n * D], ALU.mult).then_inc(weighed, 1)

            run_skewed(dve, N_GRP, [(0, logit), (1, weigh)])
            dve.wait_ge(summed, N_GRP + BUFS)
            dve.tensor_reduce(m.gq[:, :], total.rearrange("p (n d) -> p d n", d=D), AX.X, ALU.add).then_inc(done, 1)


def build_key(nc, m):
    b = Softmax(m)
    with ExitStack() as ctx:
        (k_ready, r_ready, logits, exped, weighed, divided, summed, step, done) = new_semaphores(
            nc, ctx, "k", "k_ready r_ready logits exped weighed divided summed step done")
        loaded = [ctx.enter_context(nc.semaphore(f"k_loaded{p}")) for p in range(BUFS)]
        k = [m.ps[:, p, :] for p in range(BUFS)]
        total = m.ps[:, 2, :]
        exps, divide, sum_up = softmax_stages(nc, m, b, (logits, exped, weighed, divided, summed), k, total)
        block = ctx.enter_context(nc.Block())

        @block.sync
        def _(sp):
            def load(g, p, pair):
                n, at = group_size(g), g * GRP
                sp.wait_ge(k_ready, g + 1)
                sp.dma_start(b.xT[p][:, 0:n * D], m.work[:, bass.ds(at * D, n * D)]).then_inc(loaded[p], 16)

            run_skewed(sp, N_GRP, [(0, load)])

        @block.tensor
        def _(pe):
            pe.sem_inc(k_ready, BUFS)
            pe.sem_inc(summed, BUFS)

            def project(g, p, pair):
                pe.wait_ge(loaded[p], pair * 16 + 16)
                pe.wait_ge(r_ready, g + 1)
                for j in range(group_size(g)):
                    last = pe.matmul(k[p][:, j * D:(j + 1) * D], b.xT[p][:, j * D:(j + 1) * D], m.attn_w[:, 1, :],
                                     start=True, stop=True)
                last.then_inc(k_ready, 1)

            run_skewed(pe, N_GRP, [(0, project), (3, sum_up(pe))])

        @block.scalar
        def _(act):
            act.sem_inc(exped, BUFS)
            run_skewed(act, N_GRP, [(0, exps(act))])

        @block.gpsimd
        def _(pool):
            run_skewed(pool, N_GRP, [(0, divide(pool))])

        @block.vector
        def _(dve):
            dve.sem_inc(r_ready, BUFS)
            dve.sem_inc(logits, BUFS)
            dve.sem_inc(weighed, BUFS)

            def logit(g, p, pair):
                n = group_size(g)
                r, s = (blocks_of(x[p][:, 0:n * D], n) for x in (b.r, b.s))
                dve.wait_ge(k_ready, g + 1 + BUFS)
                dve.wait_ge(exped, g + 1)
                dve.wait_ge(weighed, g + 1)
                dve.tensor_tensor(r, blocks_of(k[p][:, 0:n * D], n), bcast_mid(m.gq[:, :], n), ALU.mult).then_inc(r_ready, 1)
                dve.wait_ge(r_ready, g + 1 + BUFS)
                dve.tensor_tensor(s, r, bcast_mid(m.betab[:, :], n), ALU.mult).then_inc(step, 1)
                dve.wait_ge(step, g + 1)
                dve.tensor_reduce(b.neg_max[p][:, 0:n], s, AX.X, ALU.max, negate=True).then_inc(logits, 1)

            def weigh(g, p, pair):
                n = group_size(g)
                dve.wait_ge(exped, g + 1 + BUFS)
                dve.wait_ge(summed, g + 1)
                dve.reciprocal(b.rec[p][:, 0:n], b.sum[p][:, 0:n])
                dve.tensor_tensor(b.w[p][:, 0:n * D], b.e[p][:, 0:n * D], b.r[p][:, 0:n * D], ALU.mult).then_inc(weighed, 1)

            run_skewed(dve, N_GRP, [(0, logit), (1, weigh)])
            dve.wait_ge(summed, N_GRP + BUFS)
            dve.tensor_reduce(m.gk[:, :], total.rearrange("p (n d) -> p d n", d=D), AX.X, ALU.add).then_inc(done, 1)


def build_value(nc, m):
    with ExitStack() as ctx:
        (gate, gk_turned, gk_copied, v_ready, kv_ready, o_ready, step, added, root_done) = new_semaphores(
            nc, ctx, "v", "gate gk_turned gk_copied v_ready kv_ready o_ready step added root_done")
        v = [m.ps[:, p, :] for p in range(BUFS)]
        out = [m.ps[:, 2 + p, :] for p in range(BUFS)]
        gk_ps = m.ps[:, 4, 0:P]
        gkT = m.scratch[:, 0:P]
        kv = [m.scratch[:, P + p * BANK:P + (p + 1) * BANK] for p in range(BUFS)]
        block = ctx.enter_context(nc.Block())

        @block.tensor
        def _(pe):
            pe.sem_inc(v_ready, BUFS)
            pe.sem_inc(o_ready, BUFS)
            pe.transpose(gk_ps, m.gk[:, :], m.ident[:, :]).then_inc(gk_turned, 1)

            def value(g, p, pair):
                n, at = group_size(g), g * GRP
                pe.wait_ge(kv_ready, g + 1)
                pe.matmul(v[p][:, 0:n * D], m.attn_w[:, 2, :], m.work[:, bass.ds(at * D, n * D)],
                          start=True, stop=True).then_inc(v_ready, 1)

            def out_project(g, p, pair):
                pe.wait_ge(kv_ready, g + 1 + BUFS)
                pe.wait_ge(added, g + 1)
                for j in range(group_size(g)):
                    last = pe.matmul(out[p][:, j * D:(j + 1) * D], kv[p][:, j * D:(j + 1) * D], m.attn_w[:, 3, :],
                                     start=True, stop=True)
                last.then_inc(o_ready, 1)

            run_skewed(pe, N_GRP, [(0, value), (1, out_project)])

        @block.vector
        def _(dve):
            dve.sem_inc(kv_ready, BUFS)
            dve.sem_inc(added, BUFS)
            dve.wait_ge(gk_turned, 1)
            dve.tensor_copy(gkT, gk_ps).then_inc(gk_copied, 1)
            dve.wait_ge(gk_copied, 1)

            def times_key(g, p, pair):
                n = group_size(g)
                dve.wait_ge(v_ready, g + 1 + BUFS)
                dve.wait_ge(o_ready, g + 1)
                dve.tensor_tensor(blocks_of(kv[p][:, 0:n * D], n), blocks_of(v[p][:, 0:n * D], n),
                                  bcast_mid(gkT, n), ALU.mult).then_inc(kv_ready, 1)

            def add(g, p, pair):
                n = group_size(g)
                hg = m.h[:, bass.ds(g * GRP, n), :]
                dve.wait_ge(o_ready, g + 1 + BUFS)
                dve.tensor_tensor(hg, hg, blocks_of(out[p][:, 0:n * D], n), ALU.add).then_inc(added, 1)
                dve.wait_ge(added, g + 1 + BUFS)
                group_statistics(dve, m, g * GRP, n, step, g * 3, gate)

            run_skewed(dve, N_GRP, [(0, times_key), (2, add)])
            reciprocal_deviations(nc, dve, None, m, step, root_done, 3 * N_GRP)

        @block.scalar
        def _(act):
            reciprocal_deviations(nc, None, act, m, step, root_done, 3 * N_GRP)


TOP_STEPS = (2, 3)
PAIR_STEP, INDEX_STEP = 4, 5


def build_experts(nc, m, table, out):
    with ExitStack() as ctx:
        (xn_made, x_turned, x_copied, q_made, q_biased, scored, keys_step, picked, weight_in,
         weights_exped, found, dots, gelu_in, tanhed, valued, diag_made, rows_used, gathering,
         sum_read, stored, dve_gate) = new_semaphores(
            nc, ctx, "x", "xn_made x_turned x_copied q_made q_biased scored keys_step picked weight_in "
            "weights_exped found dots gelu_in tanhed valued diag_made rows_used gathering "
            "sum_read stored dve_gate")
        rows_in = [ctx.enter_context(nc.semaphore(f"x_rows_in{h}")) for h in range(HEADS)]

        rows = m.work[:, 0:HEADS * TOPK * ROW].rearrange("p (s r) -> p s r", r=ROW)
        o = 0

        def take(n, dtype=F32):
            nonlocal o
            o += n
            assert o <= SCRATCH
            ap = m.scratch[:, o - n:o]
            return ap if dtype == F32 else ap.bitcast(dtype)

        xn = [take(D) for _ in range(2)]
        xT = take(P)
        qT = take(HEADS * P)
        best = take(2 * HEADS * TOPK)
        best_no = take(2 * HEADS * TOPK, U32)
        cand = take(HEADS * N_CAND)
        cand_expert = take(HEADS * N_CAND)
        top = take(HEADS * TOPK)
        top_no = take(HEADS * TOPK, U32)
        hit = take(HEADS * TOPK * N_CAND)
        expert = take(HEADS * TOPK)
        experts = [take(HEADS * TOPK, U32) for _ in range(2)]
        wexp = take(HEADS * TOPK)
        wsum = take(HEADS)
        weight = [take(HEADS * TOPK) for _ in range(2)]
        dot = take(HEADS * TOPK)
        square = take(TOPK)
        gin = take(2 * TOPK)
        th = take(2 * TOPK)
        half_xw = take(2 * TOPK)
        value = take(2 * TOPK)
        diag = take(2 * TOPK * P)

        x_ps = m.ps[:, 0, 0:P]
        q_ps = m.ps[:, 1:3, :].rearrange("p b (h i) -> p (b h) i", i=P)
        s_ps = m.ps[:, 3:7, :].rearrange("p b (h e) -> p (b h) e", e=EXP)
        up_ps = m.ps[:, 7, 0:D]

        def positions(eng, step, skip_last_choice=False):
            last_pair = N_POS // 2 - 1
            with eng.Fori(0, last_pair) as pair:
                for u in range(2):
                    step(pair * 2 + u, u, True)
            step(2 * last_pair, 0, True)
            step(2 * last_pair + 1, 1, False)

        block = ctx.enter_context(nc.Block())

        @block.sync
        def _(sp):
            with sp.Fori(0, N_POS // 2) as pair:
                sp.wait_ge(sum_read, pair * 2 + 3)
                sp.dma_start(out[:, bass.ds(pair * 2, 2), :], m.h[:, bass.ds(pair * 2, 2), :]).then_inc(stored, 16)
            sp.wait_ge(stored, 16 * (N_POS // 2))

        @block.gpsimd
        def _(pool):
            def gather(n, u, _next):
                for head in range(HEADS):
                    if head == 0:
                        wait_at_gate(pool, found, n + 1, gathering)
                    wait_at_gate(pool, rows_used, n * HEADS + (head + 1), gathering)
                    for r in range(head * TOPK, (head + 1) * TOPK):
                        pool.indirect_dma_start(out=rows[:, r, :], out_offset=None, in_=table,
                                                in_offset=bass.IndirectOffsetOnAxis(ap=experts[u][:, r:r + 1], axis=0)
                                                ).then_inc(rows_in[head], 16)

            positions(pool, gather)

        @block.scalar
        def _(act):
            def queries(n):
                act.wait_ge(x_turned, n + 1)
                nc.scalar.activation(xT, x_ps, ACT.Copy).then_inc(x_copied, 1)
                act.wait_ge(q_made, n + 1)
                act.wait_ge(scored, n + 1)
                for head in range(HEADS):
                    last = nc.scalar.activation(qT[:, head * P:(head + 1) * P], q_ps[:, head, :], ACT.Identity,
                                                bias=m.bq[:, head:head + 1])
                last.then_inc(q_biased, 1)

            def pair_weights(n):
                act.wait_ge(weight_in, n + 1)
                nc.scalar.activation(wexp, wexp, ACT.Exp).then_inc(weights_exped, 1)

            def step(n, u, has_next):
                for head in range(HEADS):
                    k = head % 2
                    if head == 0 and has_next:
                        queries(n + 1)
                    act.wait_ge(gelu_in, n * HEADS + (head + 1))
                    nc.scalar.activation(th[:, k * TOPK:(k + 1) * TOPK], gin[:, k * TOPK:(k + 1) * TOPK], ACT.Tanh,
                                         scale=GELU_C * GELU_K).then_inc(tanhed, 1)
                    act.wait_ge(valued, n * HEADS + (head + 1))
                    act.wait_ge(rows_used, n * HEADS + (head - 1 + HEADS))
                    for r in range(TOPK):
                        i = k * TOPK + r
                        last = nc.scalar.activation(diag[:, i * P:(i + 1) * P], m.ident[:, :], ACT.Copy,
                                                    scale=value[:, i:i + 1])
                    last.then_inc(diag_made, 1)
                    if head == PAIR_STEP and has_next:
                        pair_weights(n + 1)

            act.sem_inc(diag_made, 2)
            queries(0)
            pair_weights(0)
            positions(act, step)

        @block.tensor
        def _(pe):
            pe.sem_inc(scored, 1)
            pe.sem_inc(rows_used, HEADS)

            def score(n, u):
                pe.wait_ge(xn_made, n + 1)
                pe.transpose(x_ps, xn[u], m.ident[:, :]).then_inc(x_turned, 1)
                pe.wait_ge(x_copied, n + 1)
                for head in range(HEADS):
                    last = pe.matmul(q_ps[:, head, :], m.wqT[:, head * P:(head + 1) * P], xT, start=True, stop=True)
                last.then_inc(q_made, 1)
                pe.wait_ge(q_biased, n + 1)
                pe.wait_ge(picked, n + 1)
                for head in range(HEADS):
                    last = pe.matmul(s_ps[:, 2 * head:2 * head + 2, :], qT[:, head * P:(head + 1) * P],
                                     m.keys[:, head, :], start=True, stop=True)
                last.then_inc(scored, 1)

            def step(n, u, has_next):
                for head in range(HEADS):
                    if head == 0 and has_next:
                        score(n + 1, 1 - u)
                    if head == 0:
                        pe.wait_ge(sum_read, n + 1)
                    pe.wait_ge(diag_made, n * HEADS + (head + 3))
                    for r in range(TOPK):
                        i = (head % 2) * TOPK + r
                        last = pe.matmul(up_ps, diag[:, i * P:(i + 1) * P], rows[:, head * TOPK + r, D:ROW],
                                         start=(head == 0 and r == 0), stop=(head == HEADS - 1 and r == TOPK - 1),
                                         skip_group_check=True)
                    last.then_inc(rows_used, 1)

            score(0, 0)
            positions(pe, step)

        @block.vector
        def _(dve):
            dve.sem_inc(picked, 1)
            dve.sem_inc(sum_read, 1)
            KEYS_STEPS = 9

            def normalise(n, u):
                dve.tensor_scalar(xn[u], m.h[:, n, :], m.stat[:, n, 0:1], m.rstd[:, bass.ds(n, 1)],
                                  ALU.subtract, ALU.mult).then_inc(xn_made, 1)

            def best_keys(n, heads):
                if heads[0] == 0:
                    wait_at_gate(dve, scored, n + 2, dve_gate)
                for i in range(2 * heads[0], 2 * heads[-1] + 2):
                    last = dve.max(best[:, i * TOPK:(i + 1) * TOPK], s_ps[:, i, :])
                last.then_inc(keys_step, 1)
                wait_at_gate(dve, keys_step, n * KEYS_STEPS + (1 if heads[0] == 0 else 2), dve_gate)
                for i in range(2 * heads[0], 2 * heads[-1] + 2):
                    last = dve.max_index(best_no[:, i * TOPK:(i + 1) * TOPK], best[:, i * TOPK:(i + 1) * TOPK], s_ps[:, i, :])
                if heads[-1] == HEADS - 1:
                    last.then_inc(picked, 1)

            def best_pairs(n):
                dve.wait_ge(picked, n + 2)
                sc = best.rearrange("p (h c r) -> p h c r", c=2, r=TOPK)
                no = best_no.rearrange("p (h c r) -> p h c r", c=2, r=TOPK)
                sums = cand.rearrange("p (h c) -> p h c", c=N_CAND)
                at = 0
                for i0, ni, nj in PAIRS:
                    for i in range(i0, i0 + ni) if nj > 1 else [i0]:
                        w = nj if nj > 1 else ni
                        shape = [P, HEADS, w]
                        rank = slice(i, i + 1) if nj > 1 else slice(i0, i0 + ni)
                        other = slice(0, nj)
                        dve.tensor_tensor(sums[:, :, at:at + w], sc[:, :, 0, rank].to_broadcast(shape),
                                          sc[:, :, 1, other].to_broadcast(shape), ALU.add)
                        last = dve.scalar_tensor_tensor(
                            out=cand_expert.rearrange("p (h c) -> p h c", c=N_CAND)[:, :, at:at + w],
                            in0=no[:, :, 0, rank].to_broadcast(shape), scalar=float(EXP),
                            in1=no[:, :, 1, other].to_broadcast(shape), op0=ALU.mult, op1=ALU.add)
                        at += w
                last.then_inc(keys_step, 1)
                wait_at_gate(dve, keys_step, n * KEYS_STEPS + 3, dve_gate)
                for head in range(HEADS):
                    last = dve.max(top[:, head * TOPK:(head + 1) * TOPK], cand[:, head * N_CAND:(head + 1) * N_CAND])
                last.then_inc(keys_step, 1)
                wait_at_gate(dve, keys_step, n * KEYS_STEPS + 4, dve_gate)
                for head in range(HEADS):
                    dve.max_index(top_no[:, head * TOPK:(head + 1) * TOPK], top[:, head * TOPK:(head + 1) * TOPK],
                                  cand[:, head * N_CAND:(head + 1) * N_CAND])
                t = top.rearrange("p (h r) -> p h r", r=TOPK)
                dve.tensor_tensor(wexp.rearrange("p (h r) -> p h r", r=TOPK), t,
                                  t[:, :, 0:1].to_broadcast([P, HEADS, TOPK]), ALU.subtract).then_inc(weight_in, 1)

            def expert_numbers(n, u):
                dve.wait_ge(weight_in, n + 1)
                hits = hit.rearrange("p (k c) -> p k c", c=N_CAND)
                dve.tensor_tensor(hits, bcast_last(top_no, N_CAND), bcast_mid(m.cand_no[:, :], HEADS * TOPK),
                                  ALU.is_equal).then_inc(keys_step, 1)
                dve.wait_ge(keys_step, n * KEYS_STEPS + 5)
                by_head = hit.rearrange("p (h k c) -> p h k c", h=HEADS, c=N_CAND)
                dve.tensor_tensor(by_head, by_head,
                                  cand_expert.rearrange("p (h c) -> p h c", c=N_CAND).unsqueeze(2)
                                  .to_broadcast([P, HEADS, TOPK, N_CAND]), ALU.mult).then_inc(keys_step, 1)
                dve.wait_ge(keys_step, n * KEYS_STEPS + 6)
                dve.tensor_reduce(expert, hits, AX.X, ALU.add).then_inc(keys_step, 1)
                dve.wait_ge(keys_step, n * KEYS_STEPS + 7)
                dve.tensor_copy(experts[u], expert).then_inc(found, 1)
                dve.wait_ge(weights_exped, n + 1)
                w = wexp.rearrange("p (h r) -> p h r", r=TOPK)
                dve.tensor_reduce(wsum, w, AX.X, ALU.add).then_inc(keys_step, 1)
                dve.wait_ge(keys_step, n * KEYS_STEPS + 8)
                dve.reciprocal(wsum, wsum).then_inc(keys_step, 1)
                dve.wait_ge(keys_step, n * KEYS_STEPS + 9)
                dve.tensor_tensor(weight[u].rearrange("p (h r) -> p h r", r=TOPK), w, bcast_last(wsum, TOPK), ALU.mult)

            def down(n, u, head):
                k = head % 2
                x = dot[:, head * TOPK:(head + 1) * TOPK]
                pair = slice(k * TOPK, (k + 1) * TOPK)
                dve.wait_ge(rows_in[head], n * (16 * TOPK) + 16 * TOPK)
                for r in range(TOPK):
                    row = rows[:, head * TOPK + r, 0:D]
                    last = dve.tensor_tensor_reduce(row, row, xn[u], 1.0, 0.0, ALU.mult, ALU.add, x[:, r:r + 1])
                last.then_inc(dots, 1)
                dve.wait_ge(dots, n * (2 * HEADS) + (2 * head + 1))
                dve.tensor_tensor(square, x, x, ALU.mult).then_inc(dots, 1)
                dve.scalar_tensor_tensor(out=half_xw[:, pair], in0=x, scalar=0.5,
                                         in1=weight[u][:, head * TOPK:(head + 1) * TOPK], op0=ALU.mult, op1=ALU.mult)
                dve.wait_ge(dots, n * (2 * HEADS) + (2 * head + 2))
                dve.scalar_tensor_tensor(out=gin[:, pair], in0=square, scalar=1.0 / GELU_K, in1=x,
                                         op0=ALU.add, op1=ALU.mult).then_inc(gelu_in, 1)

            def gelu(n, head):
                k = head % 2
                pair = slice(k * TOPK, (k + 1) * TOPK)
                dve.wait_ge(tanhed, n * HEADS + (head + 1))
                dve.wait_ge(diag_made, n * HEADS + (head + 1))
                dve.scalar_tensor_tensor(out=value[:, pair], in0=th[:, pair], scalar=1.0, in1=half_xw[:, pair],
                                         op0=ALU.add, op1=ALU.mult).then_inc(valued, 1)

            def step(n, u, has_next):
                for head in range(HEADS):
                    if head == 0 and has_next:
                        normalise(n + 1, 1 - u)
                    down(n, u, head)
                    if has_next and head in TOP_STEPS:
                        i = TOP_STEPS.index(head) * HEADS // 2
                        best_keys(n + 1, range(i, i + HEADS // 2))
                    if has_next and head == PAIR_STEP:
                        best_pairs(n + 1)
                    if has_next and head == INDEX_STEP:
                        expert_numbers(n + 1, 1 - u)
                    gelu(n, head)
                dve.wait_ge(rows_used, n * HEADS + 2 * HEADS)
                dve.tensor_tensor(m.h[:, n, :], m.h[:, n, :], up_ps, ALU.add).then_inc(sum_read, 1)

            normalise(0, 0)
            best_keys(0, range(0, HEADS // 2))
            best_keys(0, range(HEADS // 2, HEADS))
            best_pairs(0)
            expert_numbers(0, 0)
            positions(dve, step)


SCRATCH = 6600


def build(nc, x, txt, tok_wT, tok_b, cls, pos, wq, wk, wv, wr, alpha, beta, ffn_wqT, ffn_bq, keysT, table, out):
    m = Core()
    with ExitStack() as ctx:
        def sb(name, shape):
            return ctx.enter_context(nc.sbuf_tensor(name, shape, F32))

        m.h = sb("h", [P, N_POS, D])
        m.work = sb("work", [P, N_POS * D])
        m.scratch = sb("scratch", [P, SCRATCH])
        m.ident = sb("ident", [P, P])
        m.attn_w = sb("attn_w", [P, 4, D])
        m.alphab = sb("alphab", [P, D])
        m.betab = sb("betab", [P, D])
        m.wqT = sb("wqT", [P, HEADS * P])
        m.bq = sb("bq", [P, HEADS])
        m.keys = sb("keys", [P, HEADS, 2 * EXP])
        m.cand_no = sb("cand_no", [P, N_CAND])
        m.stat = sb("stat", [P, N_POS, 2])
        m.rstd = sb("rstd", [P, N_POS])
        m.newton = sb("newton", [P, N_POS])
        m.bn6 = sb("bn6", [P, GRP, 6])
        m.bn2 = sb("bn2", [P, GRP, 2])
        m.gq = sb("gq", [P, D])
        m.gk = sb("gk", [P, D])
        m.ps = ctx.enter_context(nc.psum_tensor("ps", [P, 8, BANK], F32))
        build_embed(nc, m, x, txt, tok_wT, tok_b, cls, pos, [wq, wk, wv, wr], alpha, beta, ffn_wqT, ffn_bq, keysT)
        build_statistics(nc, m)
        build_query(nc, m)
        build_key(nc, m)
        build_value(nc, m)
        build_experts(nc, m, table, out)


def kernel(**inputs):
    import numpy as np
    from concourse import bacc
    from concourse.bass_utils import run_bass_kernel_spmd

    a = {k: np.asarray(v) for k, v in inputs.items()}
    data = {
        "x": a["x"], "txt": a["txt"],
        "tok_wT": a["L0_tok_W"].reshape(D, CHUNKS, KC).transpose(2, 1, 0),
        "tok_b": a["L0_tok_b"], "cls": a["L0_tok_class_token"], "pos": a["L0_tok_pos_embed"],
        "wq": a["L0_attn_Wq"], "wk": a["L0_attn_Wk"], "wv": a["L0_attn_Wv"], "wr": a["L0_attn_Wr"],
        "alpha": a["L0_attn_alpha"], "beta": a["L0_attn_beta"],
        "ffn_wqT": a["L0_ffn_Wq"].T,
        "ffn_bq": a["L0_ffn_bq"].reshape(HEADS, P).T,
        "keysT": a["L0_ffn_keys"].transpose(1, 3, 0, 2).reshape(P, HEADS, EXP),
        "table": np.concatenate([a["L0_ffn_w_down_embed"], a["L0_ffn_w_up_embed"]], axis=1),
    }
    data = {k: np.ascontiguousarray(v) for k, v in data.items()}
    nc = bacc.Bacc("TRN2", target_bir_lowering=False, num_devices=1)
    aps = {k: nc.dram_tensor(f"in_{k}", v.shape, mybir.dt.from_np(v.dtype), kind="ExternalInput").ap()
           for k, v in data.items()}
    out = nc.dram_tensor("out_h", (P, N_POS, D), F32, kind="ExternalOutput").ap()
    build(nc, *aps.values(), out)
    r = run_bass_kernel_spmd(nc, [{f"in_{k}": v for k, v in data.items()}], core_ids=[0])
    return r.results[0]["out_h"]
```

```python
from contextlib import ExitStack

import concourse.bass as bass
from concourse import mybir

F32 = mybir.dt.float32
U32 = mybir.dt.uint32
ALU = mybir.AluOpType
ACT = mybir.ActivationFunctionType
AX = mybir.AxisListType

P = 128
D = 128
GRID, PATCH, CH = 8, 28, 3
IMG = GRID * PATCH
N_PATCH = GRID * GRID
N_TXT = 77
N_IMG_TOK = N_PATCH + 1
N_POS = N_IMG_TOK + N_TXT
EPS = 1e-5
SCALE = float(D) ** -0.5

ROWS = 4
KC = ROWS * PATCH
STRIPS = PATCH // ROWS
CHUNKS = CH * STRIPS
X_RING = 3
T_RING = 3
HALF = GRID // 2

GRP = 4
N_GRP = -(-N_POS // GRP)
BUFS = 2
BANK = 512

HEADS, TOPK, EXP = 8, 8, 128
PAIRS = [(0, 1, 8), (1, 1, 4), (2, 2, 2), (4, 4, 1)]
N_CAND = sum(ni * nj for _, ni, nj in PAIRS)
ROW = 2 * D
GELU_C = 0.7978845608028654
GELU_K = 0.044715


def group_size(g):
    return N_POS - GRP * g if isinstance(g, int) and g == N_GRP - 1 else GRP


def run_skewed(eng, count, stages):
    deepest = max(lag for lag, _ in stages)

    def step(s, parity_of_step, pair):
        for lag, fn in stages:
            if isinstance(s, int):
                if 0 <= s - lag < count:
                    fn(s - lag, (s - lag) % BUFS, (s - lag) // BUFS)
            else:
                parity = (parity_of_step - lag) % BUFS
                fn(s - lag, parity, pair - (lag + parity - parity_of_step) // BUFS)

    first = -(-deepest // BUFS) * BUFS
    last = first + (count - 1 - first) // BUFS * BUFS
    for s in range(first):
        step(s, None, None)
    with eng.Fori(first // BUFS, last // BUFS) as pair:
        for u in range(BUFS):
            step(pair * BUFS + u, u, pair)
    for s in range(last, count + deepest):
        step(s, None, None)


class Core:
    pass


def wait_at_gate(eng, sem, value, gate):
    eng.wait_ge(sem, value)
    eng.sem_inc(gate, 1)


def new_semaphores(nc, ctx, prefix, names):
    return [ctx.enter_context(nc.semaphore(f"{prefix}_{n}")) for n in names.split()]


def blocks_of(ap, n, width=D):
    return ap.rearrange("p (n d) -> p n d", d=width)


def bcast_mid(ap, n):
    return ap.unsqueeze(1).to_broadcast([ap.shape[0], n, ap.shape[1]])


def bcast_last(ap, n):
    return ap.unsqueeze(2).to_broadcast([ap.shape[0], ap.shape[1], n])


def build_embed(nc, m, x, txt, tok_wT, tok_b, cls, pos, attn_w, alpha, beta, wqT, bq, keysT):
    with ExitStack() as ctx:
        (sorted_, const_in, weights_in, zeroed, ident_made, transposed, dve_copied, act_copied,
         chunk_done, acc_read, cls_made) = new_semaphores(
            nc, ctx, "e", "sorted const_in weights_in zeroed ident_made transposed "
            "dve_copied act_copied chunk_done acc_read cls_made")
        X_CREDIT = 2 * X_RING
        x_in = [ctx.enter_context(nc.semaphore(f"e_x_in{i}")) for i in range(X_RING)]

        o = 0
        xbuf = m.work[:, o:o + X_RING * ROWS * IMG].rearrange("p (s r w) -> p s r w", s=X_RING, w=IMG)
        o += X_RING * ROWS * IMG
        xsort = m.work[:, o:o + X_RING * ROWS * IMG].rearrange("p (s g k) -> p s g k", s=X_RING, g=GRID)
        o += X_RING * ROWS * IMG
        xT = m.work[:, o:o + T_RING * GRID * P].rearrange("p (s g b) -> p s g b", s=T_RING, b=P)
        o += T_RING * GRID * P
        posb = m.work[:, o:o + N_IMG_TOK * D].rearrange("p (n d) -> p n d", d=D)
        wT = m.scratch[0:KC, 0:CHUNKS * D].rearrange("p (k d) -> p k d", d=D)
        o = CHUNKS * D
        ones = m.scratch[0:1, o:o + P]
        bias4 = m.scratch[0:1, o + P:o + P + BANK]
        clsb = m.scratch[:, o + P + BANK:o + P + BANK + D]
        acc = m.ps[:, 0:2, :]
        tp = m.ps[0:KC, 2:2 + 2 * T_RING, :]
        x_v = x.rearrange("b c (g s r) w -> b c g s (r w)", g=GRID, r=ROWS)
        N_CONST = 5

        block = ctx.enter_context(nc.Block())

        @block.sync
        def _(sp):
            sp.dma_start(wT, tok_wT).then_inc(const_in, 16)
            sp.dma_start(posb, pos.rearrange("n d -> (n d)").partition_broadcast(P)
                         .rearrange("p (n d) -> p n d", d=D)).then_inc(const_in, 16)
            for r in range(4):
                sp.dma_start(bias4[:, r * D:(r + 1) * D], tok_b.rearrange("(a d) -> a d", a=1)).then_inc(const_in, 16)
            sp.dma_start(clsb, cls.rearrange("a d -> (a d)").partition_broadcast(P)).then_inc(const_in, 16)
            with sp.Fori(0, GRID) as gy:
                for k in range(CHUNKS):
                    sp.wait_ge(sorted_, gy * CHUNKS + (k + 1))
                    sp.dma_start(xbuf[:, k % X_RING].rearrange("p r w -> p (r w)"),
                                 x_v[:, k // STRIPS, gy, k % STRIPS, :]).then_inc(x_in[k % X_RING], 16)

        @block.scalar
        def _(act):
            act.dma_start(m.h[:, N_IMG_TOK:N_POS, :], txt).then_inc(weights_in, 16)
            for n, w in enumerate(attn_w):
                act.dma_start(m.attn_w[:, n, :], w).then_inc(weights_in, 16)
            act.dma_start(m.alphab[:, :], alpha.partition_broadcast(P)).then_inc(weights_in, 16)
            act.dma_start(m.betab[:, :], beta.partition_broadcast(P)).then_inc(weights_in, 16)
            act.dma_start(m.wqT[:, :], wqT).then_inc(weights_in, 16)
            act.dma_start(m.bq[:, :], bq).then_inc(weights_in, 16)
            act.wait_ge(zeroed, 1)
            for half in range(2):
                act.dma_start(m.keys[64 * half:64 * half + 64, :, EXP * half:EXP * half + EXP],
                              keysT[64 * half:64 * half + 64]).then_inc(weights_in, 16)
            act.sem_inc(act_copied, T_RING)
            with act.Fori(0, GRID) as gy:
                for k in range(CHUNKS):
                    n = gy * CHUNKS + k
                    act.wait_ge(transposed, n * 2 + (X_CREDIT + 2))
                    act.wait_ge(chunk_done, n + 1)
                    nc.scalar.activation(xT[0:KC, k % T_RING, HALF:GRID, :],
                                         blocks_of(tp[:, 2 * (k % T_RING) + 1, :], HALF), ACT.Copy).then_inc(act_copied, 1)
            act.wait_ge(weights_in, 16 * (5 + len(attn_w) + 2))

        @block.gpsimd
        def _(pool):
            pool.memset(m.keys[:, :, :], 0.0).then_inc(zeroed, 1)
            pool.memset(m.ident[:, :], 0.0).then_inc(zeroed, 1)
            pool.wait_ge(zeroed, 2)
            pool.affine_select(out=m.ident[:, :], in_=m.ident[:, :], compare_op=ALU.not_equal, fill=1.0,
                               base=0, pattern=[[-1, P]], channel_multiplier=1).then_inc(ident_made, 1)
            pool.memset(ones, 1.0).then_inc(ident_made, 1)
            pool.iota(m.count[:, :], pattern=[[1, EXP]], base=0, channel_multiplier=0,
                      allow_small_or_imprecise_dtypes=True)

        @block.tensor
        def _(pe):
            pe.sem_inc(transposed, X_CREDIT)
            pe.sem_inc(chunk_done, T_RING)
            pe.wait_ge(ident_made, 2)
            pe.wait_ge(const_in, 16 * (N_CONST + 2))

            def transposes(gy, k, half):
                n = gy * CHUNKS + k
                pe.wait_ge([dve_copied, act_copied][half], n + 1)
                for g in range(HALF):
                    gx = HALF * half + g
                    last = pe.transpose(tp[:, 2 * (k % T_RING) + half, g * P:(g + 1) * P],
                                        xsort[:, k % X_RING, gx, :], m.ident[:, :])
                last.then_inc(transposed, 1)

            def products(gy, k):
                n = gy * CHUNKS + k
                pe.wait_ge(dve_copied, n + 1 + T_RING)
                pe.wait_ge(act_copied, n + 1 + T_RING)
                for g in range(GRID):
                    last = pe.matmul(acc[:, g // HALF, (g % HALF) * D:(g % HALF + 1) * D],
                                     xT[0:KC, k % T_RING, g, :], wT[:, k, :], start=False,
                                     stop=(k == CHUNKS - 1 and g % HALF == HALF - 1), skip_group_check=True)
                last.then_inc(chunk_done, 1)

            with pe.Fori(0, GRID) as gy:
                pe.wait_ge(acc_read, gy + 1)
                for b in range(2):
                    pe.matmul(acc[:, b, :], ones, bias4, start=True, stop=False, skip_group_check=True)
                for k in range(CHUNKS):
                    pe.wait_ge(sorted_, gy * CHUNKS + (k + 1 + X_RING))
                    transposes(gy, k, 0)
                    transposes(gy, k, 1)
                    if k:
                        products(gy, k - 1)
                products(gy, CHUNKS - 1)

        @block.vector
        def _(dve):
            dve.sem_inc(sorted_, X_RING)
            dve.sem_inc(dve_copied, T_RING)
            dve.sem_inc(acc_read, 1)
            dve.wait_ge(const_in, 16 * (N_CONST + 2))
            dve.tensor_tensor(m.h[:, 0, :], clsb, posb[:, 0, :], ALU.mult).then_inc(cls_made, 1)
            with dve.Fori(0, GRID) as gy:
                for k in range(CHUNKS):
                    n = gy * CHUNKS + k
                    dve.wait_ge(x_in[k % X_RING], (gy * (CHUNKS // X_RING) + (k // X_RING + 1)) * 16)
                    dve.wait_ge(transposed, n * 2 + 2)
                    dve.tensor_copy(xsort[:, k % X_RING].rearrange("p g (r w) -> p g r w", w=PATCH),
                                    xbuf[:, k % X_RING].rearrange("p r (g w) -> p g r w", w=PATCH)).then_inc(sorted_, 1)
                    dve.wait_ge(transposed, n * 2 + (X_CREDIT + 1))
                    dve.wait_ge(chunk_done, n + 1)
                    dve.tensor_copy(xT[0:KC, k % T_RING, 0:HALF, :],
                                    blocks_of(tp[:, 2 * (k % T_RING), :], HALF)).then_inc(dve_copied, 1)
                dve.wait_ge(chunk_done, gy * CHUNKS + CHUNKS + T_RING)
                for b in range(2):
                    at = gy * GRID + (1 + HALF * b)
                    last = dve.tensor_tensor(m.h[:, bass.ds(at, HALF), :], blocks_of(acc[:, b, :], HALF),
                                             posb[:, bass.ds(at, HALF), :], ALU.mult)
                last.then_inc(acc_read, 1)


def reciprocal_deviations(nc, dve, act, m, step, root_done, variances_ready):
    var, t = m.stat[:, :, 1], m.newton
    if act is not None:
        act.wait_ge(step, variances_ready + 1)
        nc.scalar.activation(m.rstd[:, :], t[:, :], ACT.Sqrt).then_inc(root_done, 1)
        return
    dve.wait_ge(step, variances_ready)
    dve.tensor_scalar(t[:, :], var, EPS, None, ALU.add).then_inc(step, 1)
    dve.wait_ge(root_done, 1)
    dve.reciprocal(m.rstd[:, :], m.rstd[:, :]).then_inc(step, 1)
    dve.wait_ge(step, variances_ready + 2)
    dve.tensor_tensor(t[:, :], t[:, :], m.rstd[:, :], ALU.mult).then_inc(step, 1)
    dve.wait_ge(step, variances_ready + 3)
    dve.tensor_tensor(t[:, :], t[:, :], m.rstd[:, :], ALU.mult).then_inc(step, 1)
    dve.wait_ge(step, variances_ready + 4)
    dve.tensor_scalar(t[:, :], t[:, :], -0.5, 1.5, ALU.mult, ALU.add).then_inc(step, 1)
    dve.wait_ge(step, variances_ready + 5)
    dve.tensor_tensor(m.rstd[:, :], m.rstd[:, :], t[:, :], ALU.mult).then_inc(step, 1)
    dve.wait_ge(step, variances_ready + 6)


def group_statistics(dve, m, at, n, step, before, gate):
    dve.sem_inc(gate, 1)
    for j in range(n):
        last = dve.bn_stats(m.bn6[:, j, :], m.h[:, at + j, :])
    last.then_inc(step, 1)
    wait_at_gate(dve, step, before + 1, gate)
    for j in range(n):
        last = dve.bn_aggr(m.bn2[:, j, :], m.bn6[:, j, :])
    last.then_inc(step, 1)
    dve.wait_ge(step, before + 2)
    dve.tensor_copy(m.stat[:, bass.ds(at, n), :], m.bn2[:, 0:n, :]).then_inc(step, 1)


def build_statistics(nc, m):
    with ExitStack() as ctx:
        step, root_done, gate = new_semaphores(nc, ctx, "n", "step root_done gate")
        block = ctx.enter_context(nc.Block())

        @block.vector
        def _(dve):
            dve.tensor_scalar(m.alphab[:, :], m.alphab[:, :], SCALE, None, ALU.mult)
            dve.tensor_scalar(m.betab[:, :], m.betab[:, :], SCALE, None, ALU.mult)
            with dve.Fori(0, N_GRP - 1) as g:
                group_statistics(dve, m, g * GRP, GRP, step, g * 3, gate)
            group_statistics(dve, m, (N_GRP - 1) * GRP, group_size(N_GRP - 1), step, 3 * (N_GRP - 1), gate)
            reciprocal_deviations(nc, dve, None, m, step, root_done, 3 * N_GRP)

        @block.scalar
        def _(act):
            reciprocal_deviations(nc, None, act, m, step, root_done, 3 * N_GRP)


class Softmax:

    def __init__(self, m):
        o = 0

        def take(n):
            nonlocal o
            o += n
            return m.scratch[:, o - n:o]

        self.xn = [take(BANK) for _ in range(BUFS)]
        self.xT = [take(BANK) for _ in range(BUFS)]
        self.s = [take(BANK) for _ in range(BUFS)]
        self.e = [take(BANK) for _ in range(BUFS)]
        self.r = [take(BANK) for _ in range(BUFS)]
        self.w = [take(BANK) for _ in range(BUFS)]
        self.neg_max = [take(GRP) for _ in range(BUFS)]
        self.sum = [take(GRP) for _ in range(BUFS)]
        self.rec = [take(GRP) for _ in range(BUFS)]
        assert o <= m.small


def softmax_stages(nc, m, b, sems, r_bank, total):
    (logits, exped, weighed, divided, summed) = sems

    def exps(act):
        def fn(g, p, pair):
            act.wait_ge(logits, g + 1 + BUFS)
            act.wait_ge(weighed, g + 1)
            for j in range(group_size(g)):
                last = nc.scalar.activation(b.e[p][:, j * D:(j + 1) * D], b.s[p][:, j * D:(j + 1) * D], ACT.Exp,
                                            bias=b.neg_max[p][:, j:j + 1], accum_out=b.sum[p][:, j:j + 1])
            last.then_inc(exped, 1)
        return fn

    def divide(pool):
        def fn(g, p, pair):
            n = group_size(g)
            pool.wait_ge(weighed, g + 1 + BUFS)
            w = blocks_of(b.w[p][:, 0:n * D], n)
            pool.tensor_tensor(w, w, bcast_last(b.rec[p][:, 0:n], D), ALU.mult).then_inc(divided, 1)
        return fn

    def sum_up(pe):
        def fn(g, p, pair):
            n = group_size(g)
            pe.wait_ge(divided, g + 1)
            pe.matmul(total[:, 0:n * D], m.ident[:, :], b.w[p][:, 0:n * D], start=isinstance(g, int) and g == 0,
                      stop=isinstance(g, int) and g == N_GRP - 1, skip_group_check=True).then_inc(summed, 1)
        return fn

    return exps, divide, sum_up


def build_query(nc, m):
    b = Softmax(m)
    with ExitStack() as ctx:
        (normed, norm_step, turned, copied, projected, logits, exped, weighed, divided, summed,
         step, done) = new_semaphores(nc, ctx, "q", "normed norm_step turned copied projected logits "
                                      "exped weighed divided summed step done")
        saved = [ctx.enter_context(nc.semaphore(f"q_saved{p}")) for p in range(BUFS)]
        turn = [m.ps[:, p, :] for p in range(BUFS)]
        q = [m.ps[:, 2 + p, :] for p in range(BUFS)]
        total = m.ps[:, 4, :]
        exps, divide, sum_up = softmax_stages(nc, m, b, (logits, exped, weighed, divided, summed), q, total)
        block = ctx.enter_context(nc.Block())

        @block.gpsimd
        def _(pool):
            def norm(g, p, pair):
                n, at = group_size(g), g * GRP
                x = blocks_of(b.xn[p][:, 0:n * D], n)
                pool.wait_ge(turned, g + 1)
                pool.tensor_tensor(x, m.h[:, bass.ds(at, n), :],
                                   m.stat[:, bass.ds(at, n), 0:1].to_broadcast([P, n, D]), ALU.subtract).then_inc(norm_step, 1)
                pool.wait_ge(norm_step, g + 1)
                pool.tensor_tensor(x, x, m.rstd[:, bass.ds(at, n)].unsqueeze(2).to_broadcast([P, n, D]),
                                   ALU.mult).then_inc(normed, 1)

            run_skewed(pool, N_GRP, [(0, norm), (2, divide(pool))])

        @block.sync
        def _(sp):
            for p in range(BUFS):
                sp.sem_inc(saved[p], 16)

            def save(g, p, pair):
                n, at = group_size(g), g * GRP
                sp.wait_ge(copied, g + 1 + BUFS)
                sp.dma_start(m.work[:, bass.ds(at * D, n * D)], b.xT[p][:, 0:n * D]).then_inc(saved[p], 16)

            run_skewed(sp, N_GRP, [(0, save)])
            for p in range(BUFS):
                sp.wait_ge(saved[p], 16 * (1 + N_GRP // BUFS))

        @block.scalar
        def _(act):
            act.sem_inc(copied, BUFS)
            act.sem_inc(exped, BUFS)

            def copy(g, p, pair):
                n = group_size(g)
                act.wait_ge(turned, g + 1 + BUFS)
                act.wait_ge(projected, g + 1)
                act.wait_ge(saved[p], pair * 16 + 16)
                nc.scalar.activation(b.xT[p][:, 0:n * D], turn[p][:, 0:n * D], ACT.Copy).then_inc(copied, 1)

            run_skewed(act, N_GRP, [(0, copy), (1, exps(act))])

        @block.tensor
        def _(pe):
            pe.sem_inc(turned, BUFS)
            pe.sem_inc(projected, BUFS)
            pe.sem_inc(summed, BUFS)

            def turn_over(g, p, pair):
                pe.wait_ge(normed, g + 1)
                pe.wait_ge(copied, g + 1)
                for j in range(group_size(g)):
                    last = pe.transpose(turn[p][:, j * D:(j + 1) * D], b.xn[p][:, j * D:(j + 1) * D], m.ident[:, :])
                last.then_inc(turned, 1)

            def project(g, p, pair):
                pe.wait_ge(copied, g + 1 + BUFS)
                pe.wait_ge(weighed, g + 1)
                for j in range(group_size(g)):
                    last = pe.matmul(q[p][:, j * D:(j + 1) * D], b.xT[p][:, j * D:(j + 1) * D], m.attn_w[:, 0, :],
                                     start=True, stop=True)
                last.then_inc(projected, 1)

            run_skewed(pe, N_GRP, [(0, turn_over), (1, project), (3, sum_up(pe))])

        @block.vector
        def _(dve):
            dve.sem_inc(logits, BUFS)
            dve.sem_inc(weighed, BUFS)

            def logit(g, p, pair):
                n = group_size(g)
                s = blocks_of(b.s[p][:, 0:n * D], n)
                dve.wait_ge(projected, g + 1 + BUFS)
                dve.wait_ge(exped, g + 1)
                dve.tensor_tensor(s, blocks_of(q[p][:, 0:n * D], n), bcast_mid(m.alphab[:, :], n), ALU.mult).then_inc(step, 1)
                dve.wait_ge(step, g + 1)
                dve.tensor_reduce(b.neg_max[p][:, 0:n], s, AX.X, ALU.max, negate=True).then_inc(logits, 1)

            def weigh(g, p, pair):
                n = group_size(g)
                hg = m.h[:, bass.ds(g * GRP, n), :]
                q_g = blocks_of(q[p][:, 0:n * D], n)
                dve.wait_ge(exped, g + 1 + BUFS)
                dve.wait_ge(summed, g + 1)
                dve.reciprocal(b.rec[p][:, 0:n], b.sum[p][:, 0:n])
                dve.tensor_tensor(hg, hg, q_g, ALU.add)
                dve.tensor_tensor(b.w[p][:, 0:n * D], b.e[p][:, 0:n * D], q[p][:, 0:n * D], ALU.mult).then_inc(weighed, 1)

            run_skewed(dve, N_GRP, [(0, logit), (1, weigh)])
            dve.wait_ge(summed, N_GRP + BUFS)
            dve.tensor_reduce(m.gq[:, :], total.rearrange("p (n d) -> p d n", d=D), AX.X, ALU.add).then_inc(done, 1)


def build_key(nc, m):
    b = Softmax(m)
    with ExitStack() as ctx:
        (k_ready, r_ready, logits, exped, weighed, divided, summed, step, done) = new_semaphores(
            nc, ctx, "k", "k_ready r_ready logits exped weighed divided summed step done")
        loaded = [ctx.enter_context(nc.semaphore(f"k_loaded{p}")) for p in range(BUFS)]
        k = [m.ps[:, p, :] for p in range(BUFS)]
        total = m.ps[:, 2, :]
        exps, divide, sum_up = softmax_stages(nc, m, b, (logits, exped, weighed, divided, summed), k, total)
        block = ctx.enter_context(nc.Block())

        @block.sync
        def _(sp):
            def load(g, p, pair):
                n, at = group_size(g), g * GRP
                sp.wait_ge(k_ready, g + 1)
                sp.dma_start(b.xT[p][:, 0:n * D], m.work[:, bass.ds(at * D, n * D)]).then_inc(loaded[p], 16)

            run_skewed(sp, N_GRP, [(0, load)])

        @block.tensor
        def _(pe):
            pe.sem_inc(k_ready, BUFS)
            pe.sem_inc(summed, BUFS)

            def project(g, p, pair):
                pe.wait_ge(loaded[p], pair * 16 + 16)
                pe.wait_ge(r_ready, g + 1)
                for j in range(group_size(g)):
                    last = pe.matmul(k[p][:, j * D:(j + 1) * D], b.xT[p][:, j * D:(j + 1) * D], m.attn_w[:, 1, :],
                                     start=True, stop=True)
                last.then_inc(k_ready, 1)

            run_skewed(pe, N_GRP, [(0, project), (3, sum_up(pe))])

        @block.scalar
        def _(act):
            act.sem_inc(exped, BUFS)
            run_skewed(act, N_GRP, [(0, exps(act))])

        @block.gpsimd
        def _(pool):
            run_skewed(pool, N_GRP, [(0, divide(pool))])

        @block.vector
        def _(dve):
            dve.sem_inc(r_ready, BUFS)
            dve.sem_inc(logits, BUFS)
            dve.sem_inc(weighed, BUFS)

            def logit(g, p, pair):
                n = group_size(g)
                r, s = (blocks_of(x[p][:, 0:n * D], n) for x in (b.r, b.s))
                dve.wait_ge(k_ready, g + 1 + BUFS)
                dve.wait_ge(exped, g + 1)
                dve.wait_ge(weighed, g + 1)
                dve.tensor_tensor(r, blocks_of(k[p][:, 0:n * D], n), bcast_mid(m.gq[:, :], n), ALU.mult).then_inc(r_ready, 1)
                dve.wait_ge(r_ready, g + 1 + BUFS)
                dve.tensor_tensor(s, r, bcast_mid(m.betab[:, :], n), ALU.mult).then_inc(step, 1)
                dve.wait_ge(step, g + 1)
                dve.tensor_reduce(b.neg_max[p][:, 0:n], s, AX.X, ALU.max, negate=True).then_inc(logits, 1)

            def weigh(g, p, pair):
                n = group_size(g)
                dve.wait_ge(exped, g + 1 + BUFS)
                dve.wait_ge(summed, g + 1)
                dve.reciprocal(b.rec[p][:, 0:n], b.sum[p][:, 0:n])
                dve.tensor_tensor(b.w[p][:, 0:n * D], b.e[p][:, 0:n * D], b.r[p][:, 0:n * D], ALU.mult).then_inc(weighed, 1)

            run_skewed(dve, N_GRP, [(0, logit), (1, weigh)])
            dve.wait_ge(summed, N_GRP + BUFS)
            dve.tensor_reduce(m.gk[:, :], total.rearrange("p (n d) -> p d n", d=D), AX.X, ALU.add).then_inc(done, 1)


def build_value(nc, m, hmid):
    with ExitStack() as ctx:
        (stored, gate, gk_turned, gk_copied, v_ready, kv_ready, o_ready, step, added, root_done) = new_semaphores(
            nc, ctx, "v", "stored gate gk_turned gk_copied v_ready kv_ready o_ready step added root_done")
        v = [m.ps[:, p, :] for p in range(BUFS)]
        out = [m.ps[:, 2 + p, :] for p in range(BUFS)]
        gk_ps = m.ps[:, 4, 0:P]
        gkT = m.scratch[:, 0:P]
        kv = [m.scratch[:, P + p * BANK:P + (p + 1) * BANK] for p in range(BUFS)]
        block = ctx.enter_context(nc.Block())

        @block.sync
        def _(sp):
            def store(g, p, pair):
                n, at = group_size(g), g * GRP
                sp.wait_ge(added, g + 1 + BUFS)
                sp.dma_start(hmid[:, bass.ds(at, n), :], m.h[:, bass.ds(at, n), :]).then_inc(stored, 16)

            run_skewed(sp, N_GRP, [(0, store)])
            sp.wait_ge(stored, 16 * N_GRP)

        @block.tensor
        def _(pe):
            pe.sem_inc(v_ready, BUFS)
            pe.sem_inc(o_ready, BUFS)
            pe.transpose(gk_ps, m.gk[:, :], m.ident[:, :]).then_inc(gk_turned, 1)

            def value(g, p, pair):
                n, at = group_size(g), g * GRP
                pe.wait_ge(kv_ready, g + 1)
                pe.matmul(v[p][:, 0:n * D], m.attn_w[:, 2, :], m.work[:, bass.ds(at * D, n * D)],
                          start=True, stop=True).then_inc(v_ready, 1)

            def out_project(g, p, pair):
                pe.wait_ge(kv_ready, g + 1 + BUFS)
                pe.wait_ge(added, g + 1)
                for j in range(group_size(g)):
                    last = pe.matmul(out[p][:, j * D:(j + 1) * D], kv[p][:, j * D:(j + 1) * D], m.attn_w[:, 3, :],
                                     start=True, stop=True)
                last.then_inc(o_ready, 1)

            run_skewed(pe, N_GRP, [(0, value), (1, out_project)])

        @block.vector
        def _(dve):
            dve.sem_inc(kv_ready, BUFS)
            dve.sem_inc(added, BUFS)
            dve.wait_ge(gk_turned, 1)
            dve.tensor_copy(gkT, gk_ps).then_inc(gk_copied, 1)
            dve.wait_ge(gk_copied, 1)

            def times_key(g, p, pair):
                n = group_size(g)
                dve.wait_ge(v_ready, g + 1 + BUFS)
                dve.wait_ge(o_ready, g + 1)
                dve.tensor_tensor(blocks_of(kv[p][:, 0:n * D], n), blocks_of(v[p][:, 0:n * D], n),
                                  bcast_mid(gkT, n), ALU.mult).then_inc(kv_ready, 1)

            def add(g, p, pair):
                n = group_size(g)
                hg = m.h[:, bass.ds(g * GRP, n), :]
                dve.wait_ge(o_ready, g + 1 + BUFS)
                dve.tensor_tensor(hg, hg, blocks_of(out[p][:, 0:n * D], n), ALU.add).then_inc(added, 1)
                dve.wait_ge(added, g + 1 + BUFS)
                group_statistics(dve, m, g * GRP, n, step, g * 3, gate)

            run_skewed(dve, N_GRP, [(0, times_key), (2, add)])
            reciprocal_deviations(nc, dve, None, m, step, root_done, 3 * N_GRP)

        @block.scalar
        def _(act):
            reciprocal_deviations(nc, None, act, m, step, root_done, 3 * N_GRP)


GATHERED = 3
ROUND_POS = GATHERED + 1
ROUNDS = N_POS // ROUND_POS
TAIL_POS = N_POS - ROUNDS * ROUND_POS
STEPS = GATHERED * HEADS

PREP = dict(norm=0, top_a=2, top_b=3, pairs=4, index=5)
DENSE_PREP = dict(norm=3, top_a=5, top_b=6, pairs=7)
HALF_HEADS = HEADS // 2

CHUNK_BLOCKS = 8
BANK_BLOCKS = BANK // P
CHUNK_RING = 4
TABLE_CHUNKS = EXP // CHUNK_BLOCKS
ROUND_CHUNKS = 2 * TABLE_CHUNKS
S_BANKS = EXP // BANK_BLOCKS
HOT = 4
ITEMS = P // (2 * HOT)
DOWN_AT = {0: 3, 1: 3, 2: 3, 3: 3, 4: 2, 5: 2}
ITEMS_AT = {**dict.fromkeys(range(6, 12), 2), **dict.fromkeys(range(12, 16), 1)}
UP_AT = dict.fromkeys(range(16, 24), 2)
FIRST_ITEM_STEP = min(ITEMS_AT)


def share(table, at):
    before = sum(n for s, n in table.items() if s < at)
    return list(range(before, before + table.get(at, 0)))


assert sum(DOWN_AT.values()) == sum(UP_AT.values()) == TABLE_CHUNKS and sum(ITEMS_AT.values()) == ITEMS


class Window:

    def __init__(self, r, buf, dense=True, first=False, last=False):
        self.r, self.buf, self.dense, self.first = r, buf, dense, first
        self.tile = r * GATHERED + buf
        self.pos = r * ROUND_POS + buf
        self.next_buf = (buf + 1) % GATHERED
        self.next_round = r + 1 if buf == GATHERED - 1 else r
        self.next_pos = self.next_round * ROUND_POS + self.next_buf
        self.prep = r * ROUND_POS + (2 + buf)
        self.dense_prep = None if last or not dense or buf < GATHERED - 1 else r * ROUND_POS + (ROUND_POS + 1)
        if not dense:
            self.prep = r * ROUND_POS + (1 + buf) if buf < TAIL_POS - 1 else None


def earlier(w, head, lag):
    if w.first and w.buf == 0 and head < lag:
        return None
    return w.tile - int(head < lag), (w.buf - int(head < lag)) % GATHERED, (head - lag) % HEADS, w.tile * HEADS + (head - lag)

def last_step(lag):
    tile = ROUNDS * GATHERED + TAIL_POS - 1
    return tile, TAIL_POS - 1, HEADS - 1 - lag, tile * HEADS + HEADS - 1 - lag


def windows(eng, run):
    for buf in range(GATHERED):
        run(Window(0, buf, first=True))
    with eng.Fori(1, ROUNDS - 1) as r:
        for buf in range(GATHERED):
            run(Window(r, buf))
    for buf in range(GATHERED):
        run(Window(ROUNDS - 1, buf, last=True))
    for buf in range(TAIL_POS):
        run(Window(ROUNDS, buf, dense=False))


def build_experts(nc, m, table, down_t, up_t, hmid, out):
    with ExitStack() as ctx:
        (xn_made, x_turned, x_copied, q_made, q_biased, scored, keys_step, picked, weight_in,
         weights_exped, found) = new_semaphores(
            nc, ctx, "p", "xn_made x_turned x_copied q_made q_biased scored keys_step picked weight_in "
            "weights_exped found")
        (dots, gelu_in, tanhed, valued, diag_made, rows_used, gathering, sum_read, dve_gate) = new_semaphores(
            nc, ctx, "g", "dots gelu_in tanhed valued diag_made rows_used gathering sum_read dve_gate")
        rows_in = [ctx.enter_context(nc.semaphore(f"g_rows_in{h}")) for h in range(HEADS)]
        (split_step, split_made, split_turned, coef_made, hot_made, hot_scaled, g_made, v_done, s_made,
         s_taken, up_used, dense_read) = new_semaphores(
            nc, ctx, "d", "split_step split_made split_turned coef_made hot_made hot_scaled g_made v_done s_made "
            "s_taken up_used dense_read")
        chunk_in = [ctx.enter_context(nc.semaphore(f"d_chunk_in{i}")) for i in range(CHUNK_RING)]
        h_in = [ctx.enter_context(nc.semaphore(f"h_in{b}")) for b in range(GATHERED)]
        h_stored = [ctx.enter_context(nc.semaphore(f"h_stored{b}")) for b in range(GATHERED)]
        dense_in, dense_res_in, dense_stored = new_semaphores(nc, ctx, "h", "dense_in dense_res_in dense_stored")

        n_rows, n_v, n_ring = HEADS * TOPK * ROW, EXP * P, CHUNK_RING * CHUNK_BLOCKS * P
        assert n_rows + n_v + n_ring <= BIG
        rows = m.big[:, 0:n_rows].rearrange("p (s r) -> p s r", r=ROW)
        v = m.big[:, n_rows:n_rows + n_v].rearrange("p (b t) -> p b t", t=P)
        ring = m.big[:, n_rows + n_v:n_rows + n_v + n_ring].rearrange(
            "p (c b k) -> p c b k", c=CHUNK_RING, b=CHUNK_BLOCKS)
        o = 0

        def take(n, dtype=F32):
            nonlocal o
            o += n
            assert o <= SCRATCH, o
            ap = m.scratch[:, o - n:o]
            return ap if dtype == F32 else ap.bitcast(dtype)

        xn = [take(D) for _ in range(GATHERED + 1)]
        xT = take(P)
        dense_xT = take(P)
        qT = take(HEADS * P)
        best = take(2 * HEADS * TOPK)
        best_no = take(2 * HEADS * TOPK, U32)
        cand = take(HEADS * N_CAND)
        cand_expert = take(HEADS * N_CAND)
        top = take(HEADS * TOPK)
        top_no = take(HEADS * TOPK, U32)
        hit = take(HEADS * TOPK * N_CAND)
        expert = take(HEADS * TOPK)
        experts = [take(HEADS * TOPK, U32) for _ in range(GATHERED + 1)]
        wexp = take(HEADS * TOPK)
        wsum = take(HEADS)
        weight = [take(HEADS * TOPK) for _ in range(GATHERED + 1)]
        h_buf = [take(D) for _ in range(GATHERED)]
        dot = take(HEADS * TOPK)
        square = take(TOPK)
        gin = take(2 * TOPK)
        th = take(2 * TOPK)
        half_xw = take(2 * TOPK)
        value = take(2 * TOPK)
        diag = take(2 * TOPK * P)
        dense_h = take(D)
        dense_res = take(D)
        e1_no = take(HEADS * TOPK, U32)
        e2_no = take(HEADS * TOPK, U32)
        split = take(3 * P).rearrange("p (c n k) -> p c n k", c=3, n=2)
        coef = take(3 * P // 2).rearrange("p (c t) -> p c t", c=3)
        hot1 = [take(HOT * EXP) for _ in range(2)]
        hot2 = [take(HOT * EXP) for _ in range(2)]
        hot2w = [take(HOT * EXP) for _ in range(2)]

        x_ps = m.ps[:, 0, 0:P]
        split_ps = m.ps[:, 0, P:4 * P].rearrange("p (c t) -> p c t", c=3)
        q_ps = m.ps[:, 1, :].rearrange("p (h i) -> p h i", i=P)
        s_ps = m.ps[:, 2:4, :].rearrange("p b (h e) -> p (b h) e", e=EXP)
        up_ps = m.ps[:, 4, 0:D]
        dense_ps = m.ps[:, 5, 0:D]
        work_ps = [m.ps[:, 6 + b, :].rearrange("p (n k) -> p n k", k=P) for b in range(2)]
        S_CREDIT, ROWS_CREDIT, DIAG_CREDIT, V_CREDIT, SUM_CREDIT = 2, HEADS, 2, 2, 1
        KEYS_STEPS = 9

        block = ctx.enter_context(nc.Block())

        @block.sync
        def _(sp):
            def stream(r):
                for c in range(ROUND_CHUNKS):
                    src = down_t if c < TABLE_CHUNKS else up_t
                    at = c % TABLE_CHUNKS * CHUNK_BLOCKS * P
                    old = c - CHUNK_RING
                    if 0 <= old < TABLE_CHUNKS:
                        sp.wait_ge(s_made, r * S_BANKS + (old + 1) * (CHUNK_BLOCKS // BANK_BLOCKS))
                    else:
                        old = c if old < 0 else old - TABLE_CHUNKS + CHUNK_RING
                        sp.wait_ge(up_used, r * TABLE_CHUNKS + (old + 1))
                    sp.dma_start(ring[:, c % CHUNK_RING].rearrange("p b k -> p (b k)"),
                                 src[:, at:at + CHUNK_BLOCKS * P]).then_inc(chunk_in[c % CHUNK_RING], 16)

            with sp.Fori(0, ROUNDS) as r:
                stream(r)

        @block.gpsimd
        def _(pool):
            def gather(w):
                wait_at_gate(pool, found, w.tile + 1, gathering)
                for head in range(HEADS):
                    wait_at_gate(pool, rows_used, w.tile * HEADS + (head + 1), gathering)
                    for k in range(head * TOPK, (head + 1) * TOPK):
                        pool.indirect_dma_start(out=rows[:, k, :], out_offset=None, in_=table,
                                                in_offset=bass.IndirectOffsetOnAxis(
                                                    ap=experts[w.buf][:, k:k + 1], axis=0)).then_inc(rows_in[head], 16)

            windows(pool, gather)

        @block.scalar
        def _(act):
            def copy_turned(q, to):
                act.wait_ge(x_turned, q + 1)
                nc.scalar.activation(to, x_ps, ACT.Copy).then_inc(x_copied, 1)

            def bias_queries(q, half):
                act.wait_ge(q_made, q * 2 + (half + 1))
                act.wait_ge(scored, q * 2 + (half + 1))
                for i in range(HALF_HEADS):
                    head = half * HALF_HEADS + i
                    last = nc.scalar.activation(qT[:, head * P:(head + 1) * P], q_ps[:, i, :], ACT.Identity,
                                                bias=m.bq[:, head:head + 1])
                last.then_inc(q_biased, 1)

            def exp_weights(q):
                act.wait_ge(weight_in, q + 1)
                nc.scalar.activation(wexp, wexp, ACT.Exp).then_inc(weights_exped, 1)

            def load(b, pos):
                act.dma_start(h_buf[b], hmid[:, pos, :]).then_inc(h_in[b], 16)

            def store_and_load(w, head):
                b = (w.buf - 1) % GATHERED
                r = w.r if w.buf else w.r - 1
                if not (w.first and w.buf == 0):
                    if head == 4:
                        act.wait_ge(sum_read, w.tile + SUM_CREDIT)
                        act.dma_start(out[:, w.pos - 1 if w.buf else w.pos - 2, :], h_buf[b]).then_inc(h_stored[b], 16)
                    if head == 6 and w.dense and not (isinstance(r, int) and r == ROUNDS - 1 and b >= TAIL_POS):
                        act.wait_ge(h_stored[b], r * 16 + 16)
                        load(b, (r + 1) * ROUND_POS + b)
                if w.buf == 0 and head == 3 and not w.first:
                    act.wait_ge(dense_read, w.r + 1)
                    act.dma_start(out[:, w.pos - 1, :], dense_res).then_inc(dense_stored, 16)
                if w.buf == 0 and head == 6 and w.dense:
                    if not w.first:
                        act.wait_ge(dense_stored, w.r * 16)
                    act.dma_start(dense_res, hmid[:, w.pos + GATHERED, :]).then_inc(dense_res_in, 16)
                if w.buf == 1 and head == 4 and w.dense and not (isinstance(w.r, int) and w.r == ROUNDS - 1):
                    act.wait_ge(xn_made, w.prep)
                    act.dma_start(dense_h, hmid[:, w.pos + (ROUND_POS + GATHERED - 1), :]).then_inc(dense_in, 16)

            def take_scores(w, c):
                for b in range(c * CHUNK_BLOCKS // BANK_BLOCKS, (c + 1) * CHUNK_BLOCKS // BANK_BLOCKS):
                    act.wait_ge(s_made, w.r * S_BANKS + (b + 1))
                    nc.scalar.activation(v[:, b * BANK_BLOCKS:(b + 1) * BANK_BLOCKS, :], work_ps[b % 2][:, :, :],
                                         ACT.Gelu_apprx_tanh).then_inc(s_taken, 1)

            def scale_hot(w, c):
                act.wait_ge(hot_made, w.r * ITEMS + (c + 1))
                for i in range(HOT):
                    t = c * HOT + i
                    last = nc.scalar.activation(hot2w[c % 2][:, i * EXP:(i + 1) * EXP], hot2[c % 2][:, i * EXP:(i + 1) * EXP],
                                                ACT.Copy, scale=coef[:, 2, t:t + 1])
                last.then_inc(hot_scaled, 1)

            def tanh(w, head):
                k = head % 2
                act.wait_ge(gelu_in, w.tile * HEADS + (head + 1))
                nc.scalar.activation(th[:, k * TOPK:(k + 1) * TOPK], gin[:, k * TOPK:(k + 1) * TOPK], ACT.Tanh,
                                     scale=GELU_C * GELU_K).then_inc(tanhed, 1)

            def diagonals(tile, b, head, s):
                k = head % 2
                act.wait_ge(valued, s + 1)
                act.wait_ge(rows_used, s + (ROWS_CREDIT - 1))
                for k8 in range(TOPK):
                    i = k * TOPK + k8
                    last = nc.scalar.activation(diag[:, i * P:(i + 1) * P], m.ident[:, :], ACT.Copy,
                                                scale=value[:, i:i + 1])
                last.then_inc(diag_made, 1)

            def run(w):
                for head in range(HEADS):
                    at = w.buf * HEADS + head
                    if w.prep is not None and head == PREP["norm"]:
                        copy_turned(w.prep, xT)
                    if w.dense_prep is not None and head == DENSE_PREP["norm"]:
                        copy_turned(w.dense_prep, dense_xT)
                    down, items = (share(DOWN_AT, at), share(ITEMS_AT, at)) if w.dense else ([], [])
                    for c in down[:1]:
                        take_scores(w, c)
                    if items and items[0] == 0:
                        scale_hot(w, 0)
                    for c in items[:1]:
                        if c + 1 < ITEMS:
                            scale_hot(w, c + 1)
                    tanh(w, head)
                    if earlier(w, head, 1):
                        diagonals(*earlier(w, head, 1))
                    for c in down[1:]:
                        take_scores(w, c)
                    for c in items[1:]:
                        if c + 1 < ITEMS:
                            scale_hot(w, c + 1)
                    for prep, when in ((w.prep, PREP), (w.dense_prep, DENSE_PREP)):
                        if prep is None:
                            continue
                        if head == when["norm"]:
                            bias_queries(prep, 0)
                        if head == when["norm"] + 1:
                            bias_queries(prep, 1)
                        if head == when["pairs"]:
                            exp_weights(prep)
                    store_and_load(w, head)

            act.sem_inc(diag_made, DIAG_CREDIT)
            act.sem_inc(s_taken, S_CREDIT)
            for b in range(GATHERED):
                load(b, b)
            act.dma_start(dense_h, hmid[:, GATHERED, :]).then_inc(dense_in, 16)
            for q, to in enumerate((xT, dense_xT)):
                copy_turned(q, to)
                bias_queries(q, 0)
                bias_queries(q, 1)
                exp_weights(q)
            windows(act, run)
            diagonals(*last_step(0))
            act.wait_ge(sum_read, ROUNDS * GATHERED + TAIL_POS + SUM_CREDIT)
            act.dma_start(out[:, N_POS - 1, :], h_buf[TAIL_POS - 1]).then_inc(h_stored[TAIL_POS - 1], 16)
            for b in range(GATHERED):
                act.wait_ge(h_stored[b], 16 * (ROUNDS + (1 if b < TAIL_POS else 0)))
            act.wait_ge(dense_stored, 16 * ROUNDS)

        @block.tensor
        def _(pe):
            pe.sem_inc(scored, 2)
            pe.sem_inc(rows_used, ROWS_CREDIT)
            pe.sem_inc(up_used, CHUNK_RING)

            def turn(q, b):
                pe.wait_ge(xn_made, q + 1)
                pe.transpose(x_ps, xn[b], m.ident[:, :]).then_inc(x_turned, 1)

            def query(q, half, xT_of):
                pe.wait_ge(x_copied, q + 1)
                pe.wait_ge(q_biased, q * 2 + half) if not (isinstance(q, int) and q * 2 + half == 0) else None
                for i in range(HALF_HEADS):
                    head = half * HALF_HEADS + i
                    last = pe.matmul(q_ps[:, i, :], m.wqT[:, head * P:(head + 1) * P], xT_of, start=True, stop=True)
                last.then_inc(q_made, 1)

            def score(q, half):
                pe.wait_ge(q_biased, q * 2 + (half + 1))
                pe.wait_ge(picked, q * 2 + (half + 1))
                for i in range(HALF_HEADS):
                    head = half * HALF_HEADS + i
                    last = pe.matmul(s_ps[:, 2 * i:2 * i + 2, :], qT[:, head * P:(head + 1) * P],
                                     m.keys[:, head, :], start=True, stop=True)
                last.then_inc(scored, 1)

            def dense_down(w, c):
                pe.wait_ge(chunk_in[c % CHUNK_RING], w.r * (16 * ROUND_CHUNKS // CHUNK_RING) + 16 * (c // CHUNK_RING + 1))
                for b in range(CHUNK_BLOCKS):
                    bank, col = divmod(c * CHUNK_BLOCKS + b, BANK_BLOCKS)
                    if col == 0:
                        pe.wait_ge(s_taken, w.r * S_BANKS + (bank + 1))
                    last = pe.matmul(work_ps[bank % 2][:, col, :], ring[:, c % CHUNK_RING, b, :], dense_xT, start=True, stop=True)
                    if col == BANK_BLOCKS - 1:
                        last.then_inc(s_made, 1)

            def lay_out(w, c):
                pe.wait_ge(hot_scaled, w.r * ITEMS + (c + 1))
                if c == 0:
                    pe.wait_ge(s_taken, w.r * S_BANKS + (S_BANKS + S_CREDIT))
                for side in range(2):
                    pe.wait_ge(v_done, w.r * (2 * ITEMS) + (2 * c + side + 1))
                    part = slice(P // 2 * side, P // 2 * (side + 1))
                    for i in range(HOT):
                        last = pe.matmul(work_ps[side][:, i, :], hot1[c % 2][part, i * EXP:(i + 1) * EXP],
                                         hot2w[c % 2][part, i * EXP:(i + 1) * EXP], start=True, stop=True)
                    last.then_inc(g_made, 1)

            def dense_up(w, c):
                if c == 0:
                    pe.wait_ge(v_done, w.r * (2 * ITEMS) + (2 * ITEMS + V_CREDIT))
                    pe.wait_ge(dense_read, w.r + 1)
                n = TABLE_CHUNKS + c
                pe.wait_ge(chunk_in[n % CHUNK_RING], w.r * (16 * ROUND_CHUNKS // CHUNK_RING) + 16 * (n // CHUNK_RING + 1))
                for b in range(CHUNK_BLOCKS):
                    block_no = c * CHUNK_BLOCKS + b
                    last = pe.matmul(dense_ps, v[:, block_no, :], ring[:, n % CHUNK_RING, b, :],
                                     start=(block_no == 0), stop=(block_no == EXP - 1), skip_group_check=True)
                last.then_inc(up_used, 1)

            def head_sum(tile, b, head, s):
                if head == 0:
                    pe.wait_ge(sum_read, tile + SUM_CREDIT)
                pe.wait_ge(diag_made, s + (1 + DIAG_CREDIT))
                for k in range(TOPK):
                    i = (head % 2) * TOPK + k
                    last = pe.matmul(up_ps, diag[:, i * P:(i + 1) * P], rows[:, head * TOPK + k, D:ROW],
                                     start=(head == 0 and k == 0), stop=(head == HEADS - 1 and k == TOPK - 1),
                                     skip_group_check=True)
                last.then_inc(rows_used, 1)

            def run(w):
                for head in range(HEADS):
                    at = w.buf * HEADS + head
                    preps = [(q, when, b, xt) for q, when, b, xt in (
                        (w.prep, PREP, w.next_buf, xT), (w.dense_prep, DENSE_PREP, GATHERED, dense_xT)) if q is not None]
                    for q, when, b, xt in preps:
                        if head == when["norm"]:
                            turn(q, b)
                        if head == when["norm"] + 1:
                            score(q, 0)
                            query(q, 1, xt)
                    if w.dense:
                        if at == 1:
                            pe.wait_ge(split_made, w.r + 1)
                            for i in range(3):
                                last = pe.transpose(split_ps[:, i, :], split[:, i].rearrange("p n k -> p (n k)"), m.ident[:, :])
                            last.then_inc(split_turned, 1)
                        for c in share(DOWN_AT, at):
                            dense_down(w, c)
                        for c in share(ITEMS_AT, at)[:1]:
                            lay_out(w, c)
                        for c in share(UP_AT, at):
                            dense_up(w, c)
                    if earlier(w, head, 2):
                        head_sum(*earlier(w, head, 2))
                    if w.dense:
                        for c in share(ITEMS_AT, at)[1:]:
                            lay_out(w, c)
                    for q, when, b, xt in preps:
                        if head == when["norm"]:
                            query(q, 0, xt)
                        if head == when["top_a"]:
                            score(q, 1)

            for q, b, xt in ((0, 0, xT), (1, GATHERED, dense_xT)):
                turn(q, b)
                query(q, 0, xt)
                score(q, 0)
                query(q, 1, xt)
                score(q, 1)
            windows(pe, run)
            head_sum(*last_step(1))
            head_sum(*last_step(0))

        @block.vector
        def _(dve):
            dve.sem_inc(picked, 1)
            dve.sem_inc(sum_read, SUM_CREDIT)
            dve.sem_inc(dense_read, 1)
            dve.sem_inc(v_done, V_CREDIT)

            def normalise(h, pos, b):
                dve.tensor_scalar(xn[b], h, m.stat[:, pos, 0:1], m.rstd[:, bass.ds(pos, 1)],
                                  ALU.subtract, ALU.mult).then_inc(xn_made, 1)

            def best_keys(q, half):
                wait_at_gate(dve, scored, q * 2 + (half + 3), dve_gate)
                at = half * HALF_HEADS * 2
                for i in range(2 * HALF_HEADS):
                    last = dve.max(best[:, (at + i) * TOPK:(at + i + 1) * TOPK], s_ps[:, i, :])
                last.then_inc(keys_step, 1)
                wait_at_gate(dve, keys_step, q * KEYS_STEPS + (half + 1), dve_gate)
                for i in range(2 * HALF_HEADS):
                    j = slice((at + i) * TOPK, (at + i + 1) * TOPK)
                    last = dve.max_index(best_no[:, j], best[:, j], s_ps[:, i, :])
                last.then_inc(picked, 1)

            def best_pairs(q):
                dve.wait_ge(picked, q * 2 + 3)
                sc = best.rearrange("p (h c r) -> p h c r", c=2, r=TOPK)
                no = best_no.rearrange("p (h c r) -> p h c r", c=2, r=TOPK)
                sums = cand.rearrange("p (h c) -> p h c", c=N_CAND)
                numbers = cand_expert.rearrange("p (h c) -> p h c", c=N_CAND)
                at = 0
                for i0, ni, nj in PAIRS:
                    for i in range(i0, i0 + ni) if nj > 1 else [i0]:
                        w = nj if nj > 1 else ni
                        shape = [P, HEADS, w]
                        rank = slice(i, i + 1) if nj > 1 else slice(i0, i0 + ni)
                        dve.tensor_tensor(sums[:, :, at:at + w], sc[:, :, 0, rank].to_broadcast(shape),
                                          sc[:, :, 1, 0:nj].to_broadcast(shape), ALU.add)
                        last = dve.scalar_tensor_tensor(
                            out=numbers[:, :, at:at + w], in0=no[:, :, 0, rank].to_broadcast(shape), scalar=float(EXP),
                            in1=no[:, :, 1, 0:nj].to_broadcast(shape), op0=ALU.mult, op1=ALU.add)
                        at += w
                last.then_inc(keys_step, 1)
                wait_at_gate(dve, keys_step, q * KEYS_STEPS + 3, dve_gate)
                for head in range(HEADS):
                    last = dve.max(top[:, head * TOPK:(head + 1) * TOPK], cand[:, head * N_CAND:(head + 1) * N_CAND])
                last.then_inc(keys_step, 1)
                wait_at_gate(dve, keys_step, q * KEYS_STEPS + 4, dve_gate)
                for head in range(HEADS):
                    dve.max_index(top_no[:, head * TOPK:(head + 1) * TOPK], top[:, head * TOPK:(head + 1) * TOPK],
                                  cand[:, head * N_CAND:(head + 1) * N_CAND])
                t = top.rearrange("p (h r) -> p h r", r=TOPK)
                dve.tensor_tensor(wexp.rearrange("p (h r) -> p h r", r=TOPK), t,
                                  t[:, :, 0:1].to_broadcast([P, HEADS, TOPK]), ALU.subtract).then_inc(weight_in, 1)

            def expert_numbers(q, b, signal):
                dve.wait_ge(weight_in, q + 1)
                hits = hit.rearrange("p (k c) -> p k c", c=N_CAND)
                dve.tensor_tensor(hits, bcast_last(top_no, N_CAND), bcast_mid(m.count[:, 0:N_CAND], HEADS * TOPK),
                                  ALU.is_equal).then_inc(keys_step, 1)
                dve.wait_ge(keys_step, q * KEYS_STEPS + 5)
                by_head = hit.rearrange("p (h k c) -> p h k c", h=HEADS, c=N_CAND)
                dve.tensor_tensor(by_head, by_head,
                                  cand_expert.rearrange("p (h c) -> p h c", c=N_CAND).unsqueeze(2)
                                  .to_broadcast([P, HEADS, TOPK, N_CAND]), ALU.mult).then_inc(keys_step, 1)
                dve.wait_ge(keys_step, q * KEYS_STEPS + 6)
                dve.tensor_reduce(expert, hits, AX.X, ALU.add).then_inc(keys_step, 1)
                dve.wait_ge(keys_step, q * KEYS_STEPS + 7)
                dve.tensor_copy(experts[b], expert).then_inc(signal, 1)
                dve.wait_ge(weights_exped, q + 1)
                w = wexp.rearrange("p (h r) -> p h r", r=TOPK)
                dve.tensor_reduce(wsum, w, AX.X, ALU.add).then_inc(keys_step, 1)
                dve.wait_ge(keys_step, q * KEYS_STEPS + 8)
                dve.reciprocal(wsum, wsum).then_inc(keys_step, 1)
                dve.wait_ge(keys_step, q * KEYS_STEPS + 9)
                return dve.tensor_tensor(weight[b].rearrange("p (h r) -> p h r", r=TOPK), w, bcast_last(wsum, TOPK), ALU.mult)

            def split_pairs(w):
                expert_numbers(w.dense_q, GATHERED, split_step).then_inc(split_step, 1)
                dve.wait_ge(split_step, w.r * 3 + 2)
                number = experts[GATHERED]
                dve.tensor_scalar(e1_no, number, EXP.bit_length() - 1, None, ALU.logical_shift_right)
                dve.tensor_scalar(e2_no, number, EXP - 1, None, ALU.bitwise_and).then_inc(split_step, 1)
                dve.wait_ge(split_step, w.r * 3 + 3)
                dve.tensor_copy(split[:, 0], bcast_mid(e1_no, 2))
                dve.tensor_copy(split[:, 1], bcast_mid(e2_no, 2))
                dve.tensor_copy(split[:, 2], bcast_mid(weight[GATHERED], 2)).then_inc(split_made, 1)

            def take_coef(w):
                dve.wait_ge(split_turned, w.r + 1)
                for side in range(2):
                    part = slice(P // 2 * side, P // 2 * (side + 1))
                    last = dve.tensor_copy(coef[part], split_ps[part, :, P // 2 * side:P // 2 * (side + 1)])
                last.then_inc(coef_made, 1)

            def make_hot(w, c):
                if c == 0:
                    dve.wait_ge(coef_made, w.r + 1)
                for hot, row in ((hot1, 0), (hot2, 1)):
                    last = dve.tensor_tensor(blocks_of(hot[c % 2], HOT), bcast_mid(m.count[:, :], HOT),
                                             bcast_last(coef[:, row, c * HOT:(c + 1) * HOT], EXP), ALU.is_equal)
                last.then_inc(hot_made, 1)

            def weigh_values(w, c):
                if c == 0:
                    dve.wait_ge(s_taken, w.r * S_BANKS + (S_BANKS + S_CREDIT))
                for side in range(2):
                    dve.wait_ge(g_made, w.r * (2 * ITEMS) + (2 * c + side + 1))
                    t = P // 2 * side + c * HOT
                    values = v[:, :, t:t + HOT].rearrange("p b t -> p t b")
                    dve.tensor_tensor(values, values, work_ps[side][:, 0:HOT, :], ALU.mult).then_inc(v_done, 1)

            def item(w, c):
                if c + 1 < ITEMS:
                    make_hot(w, c + 1)
                weigh_values(w, c)

            def down(w, head):
                x = dot[:, head * TOPK:(head + 1) * TOPK]
                pair = slice((head % 2) * TOPK, (head % 2 + 1) * TOPK)
                dve.wait_ge(rows_in[head], w.tile * (16 * TOPK) + 16 * TOPK)
                for k in range(TOPK):
                    row = rows[:, head * TOPK + k, 0:D]
                    last = dve.tensor_tensor_reduce(row, row, xn[w.buf], 1.0, 0.0, ALU.mult, ALU.add, x[:, k:k + 1])
                last.then_inc(dots, 1)
                dve.wait_ge(dots, w.tile * (2 * HEADS) + (2 * head + 1))
                dve.tensor_tensor(square, x, x, ALU.mult).then_inc(dots, 1)
                dve.scalar_tensor_tensor(out=half_xw[:, pair], in0=x, scalar=0.5,
                                         in1=weight[w.buf][:, head * TOPK:(head + 1) * TOPK], op0=ALU.mult, op1=ALU.mult)
                dve.wait_ge(dots, w.tile * (2 * HEADS) + (2 * head + 2))
                dve.scalar_tensor_tensor(out=gin[:, pair], in0=square, scalar=1.0 / GELU_K, in1=x,
                                         op0=ALU.add, op1=ALU.mult).then_inc(gelu_in, 1)

            def gelu(tile, b, head, s):
                pair = slice((head % 2) * TOPK, (head % 2 + 1) * TOPK)
                dve.wait_ge(tanhed, s + 1)
                dve.wait_ge(diag_made, s + 1)
                dve.scalar_tensor_tensor(out=value[:, pair], in0=th[:, pair], scalar=1.0, in1=half_xw[:, pair],
                                         op0=ALU.add, op1=ALU.mult).then_inc(valued, 1)

            def add_sum(tiles, b):
                dve.wait_ge(rows_used, tiles * HEADS + ROWS_CREDIT)
                dve.tensor_tensor(h_buf[b], h_buf[b], up_ps, ALU.add).then_inc(sum_read, 1)

            def add_dense(rounds):
                dve.wait_ge(dense_res_in, rounds * 16)
                dve.wait_ge(up_used, rounds * TABLE_CHUNKS + CHUNK_RING)
                dve.tensor_tensor(dense_res, dense_res, dense_ps, ALU.add).then_inc(dense_read, 1)

            def run(w):
                for head in range(HEADS):
                    at = w.buf * HEADS + head
                    items = share(ITEMS_AT, at) if w.dense else []
                    if w.prep is not None and head == PREP["norm"]:
                        dve.wait_ge(h_in[w.next_buf], w.next_round * 16 + 16)
                        normalise(h_buf[w.next_buf], w.next_pos, w.next_buf)
                    if w.dense_prep is not None and head == DENSE_PREP["norm"]:
                        dve.wait_ge(dense_in, w.r * 16 + 32)
                        normalise(dense_h, w.r * ROUND_POS + (ROUND_POS + GATHERED), GATHERED)
                    for c in items[:1]:
                        item(w, c)
                    down(w, head)
                    if earlier(w, head, 1):
                        gelu(*earlier(w, head, 1))
                    if w.dense and at == 0:
                        w.dense_q = 1 if w.first else (w.r * ROUND_POS + 1)
                        split_pairs(w)
                    if w.dense and at == 2:
                        take_coef(w)
                    if w.prep is not None:
                        if head == PREP["top_a"]:
                            best_keys(w.prep, 0)
                        if head == PREP["top_b"]:
                            best_keys(w.prep, 1)
                        if head == PREP["pairs"]:
                            best_pairs(w.prep)
                        if head == PREP["index"]:
                            expert_numbers(w.prep, w.next_buf, found)
                    if w.dense_prep is not None:
                        if head == DENSE_PREP["top_a"]:
                            best_keys(w.dense_prep, 0)
                        if head == DENSE_PREP["top_b"]:
                            best_keys(w.dense_prep, 1)
                        if head == DENSE_PREP["pairs"]:
                            best_pairs(w.dense_prep)
                    if w.dense and at == FIRST_ITEM_STEP - 1:
                        make_hot(w, 0)
                    for c in items[1:]:
                        item(w, c)
                    if not (w.first and w.buf == 0):
                        if head == 1:
                            add_sum(w.tile, (w.buf - 1) % GATHERED)
                        if head == 1 and w.buf == 0:
                            add_dense(w.r)

            dve.wait_ge(h_in[0], 16)
            normalise(h_buf[0], 0, 0)
            best_keys(0, 0)
            best_keys(0, 1)
            best_pairs(0)
            expert_numbers(0, 0, found)
            dve.wait_ge(dense_in, 16)
            normalise(dense_h, GATHERED, GATHERED)
            best_keys(1, 0)
            best_keys(1, 1)
            best_pairs(1)
            windows(dve, run)
            gelu(*last_step(0))
            add_sum(ROUNDS * GATHERED + TAIL_POS, TAIL_POS - 1)


BIG = 36864
SCRATCH = 11600


def build(nc, x, txt, tok_wT, tok_b, cls, pos, wq, wk, wv, wr, alpha, beta, ffn_wqT, ffn_bq, keysT, table,
          down_t, up_t, out):
    hmid = nc.dram_tensor("hmid", (P, N_POS, D), F32, kind="Internal").ap()
    m = Core()
    with ExitStack() as ctx:
        def sb(name, shape):
            return ctx.enter_context(nc.sbuf_tensor(name, shape, F32))

        m.big = sb("big", [P, BIG])
        m.scratch = sb("scratch", [P, SCRATCH])
        m.h = m.big[:, 0:N_POS * D].rearrange("p (n d) -> p n d", d=D)
        m.work = m.big[:, N_POS * D:2 * N_POS * D]
        top = SCRATCH

        def keep(n):
            nonlocal top
            top -= n
            return m.scratch[:, top:top + n]

        m.attn_w = keep(4 * D).rearrange("p (n d) -> p n d", d=D)
        m.alphab, m.betab, m.gq, m.gk = (keep(D) for _ in range(4))
        m.newton = keep(N_POS)
        m.bn6 = keep(GRP * 6).rearrange("p (n k) -> p n k", k=6)
        m.bn2 = keep(GRP * 2).rearrange("p (n k) -> p n k", k=2)
        m.small = top
        m.ident = sb("ident", [P, P])
        m.wqT = sb("wqT", [P, HEADS * P])
        m.bq = sb("bq", [P, HEADS])
        m.keys = sb("keys", [P, HEADS, 2 * EXP])
        m.count = sb("count", [P, EXP])
        m.stat = sb("stat", [P, N_POS, 2])
        m.rstd = sb("rstd", [P, N_POS])
        m.ps = ctx.enter_context(nc.psum_tensor("ps", [P, 8, BANK], F32))
        build_embed(nc, m, x, txt, tok_wT, tok_b, cls, pos, [wq, wk, wv, wr], alpha, beta, ffn_wqT, ffn_bq, keysT)
        build_statistics(nc, m)
        build_query(nc, m)
        build_key(nc, m)
        build_value(nc, m, hmid)
        build_experts(nc, m, table, down_t, up_t, hmid, out)


def kernel(**inputs):
    import numpy as np
    from concourse import bacc
    from concourse.bass_utils import run_bass_kernel_spmd

    a = {k: np.asarray(v) for k, v in inputs.items()}
    down, up = a["L0_ffn_w_down_embed"], a["L0_ffn_w_up_embed"]
    data = {
        "x": a["x"], "txt": a["txt"],
        "tok_wT": a["L0_tok_W"].reshape(D, CHUNKS, KC).transpose(2, 1, 0),
        "tok_b": a["L0_tok_b"], "cls": a["L0_tok_class_token"], "pos": a["L0_tok_pos_embed"],
        "wq": a["L0_attn_Wq"], "wk": a["L0_attn_Wk"], "wv": a["L0_attn_Wv"], "wr": a["L0_attn_Wr"],
        "alpha": a["L0_attn_alpha"], "beta": a["L0_attn_beta"],
        "ffn_wqT": a["L0_ffn_Wq"].T,
        "ffn_bq": a["L0_ffn_bq"].reshape(HEADS, P).T,
        "keysT": a["L0_ffn_keys"].transpose(1, 3, 0, 2).reshape(P, HEADS, EXP),
        "table": np.concatenate([down, up], axis=1),
        "down_t": down.reshape(EXP, EXP, D).transpose(2, 1, 0).reshape(D, EXP * EXP),
        "up_t": up.reshape(EXP, EXP * D),
    }
    data = {k: np.ascontiguousarray(v) for k, v in data.items()}
    nc = bacc.Bacc("TRN2", target_bir_lowering=False, num_devices=1)
    aps = {k: nc.dram_tensor(f"in_{k}", v.shape, mybir.dt.from_np(v.dtype), kind="ExternalInput").ap()
           for k, v in data.items()}
    out = nc.dram_tensor("out_h", (P, N_POS, D), F32, kind="ExternalOutput").ap()
    build(nc, *aps.values(), out)
    r = run_bass_kernel_spmd(nc, [{f"in_{k}": v for k, v in data.items()}], core_ids=[0])
    return r.results[0]["out_h"]
```

```python
from contextlib import ExitStack

import concourse.bass as bass
from concourse import mybir

F32 = mybir.dt.float32
U32 = mybir.dt.uint32
ALU = mybir.AluOpType
ACT = mybir.ActivationFunctionType
AX = mybir.AxisListType

P = 128
D = 128
GRID, PATCH, CH = 8, 28, 3
IMG = GRID * PATCH
N_PATCH = GRID * GRID
N_TXT = 77
N_IMG_TOK = N_PATCH + 1
N_POS = N_IMG_TOK + N_TXT
EPS = 1e-5
SCALE = float(D) ** -0.5

ROWS = 4
KC = ROWS * PATCH
STRIPS = PATCH // ROWS
CHUNKS = CH * STRIPS
X_RING = 3
T_RING = 3
HALF = GRID // 2

PRODUCT_LAG = 2
SORT_AHEAD = 2
TXT_AT = (4, 9, 14)
TXT_PIECES = len(TXT_AT)
TXT_PIECE = N_TXT // GRID // TXT_PIECES
TXT_ROW = TXT_PIECES * TXT_PIECE
TXT_REST = N_TXT - GRID * TXT_ROW
GRP = 4
N_GRP = -(-N_POS // GRP)
BUFS = 3
BANK = 512

HEADS, TOPK, EXP = 8, 8, 128
PAIRS = [(0, 1, 8), (1, 1, 4), (2, 2, 2), (4, 4, 1)]
N_CAND = sum(ni * nj for _, ni, nj in PAIRS)
ROW = 2 * D
GELU_C = 0.7978845608028654
GELU_K = 0.044715


def group_size(g):
    return N_POS - GRP * g if isinstance(g, int) and g == N_GRP - 1 else GRP


def run_skewed(eng, count, stages):
    deepest = max(lag for lag, _ in stages)

    def step(s, parity_of_step, pair):
        for lag, fn in stages:
            if isinstance(s, int):
                if 0 <= s - lag < count:
                    fn(s - lag, (s - lag) % BUFS, (s - lag) // BUFS)
            else:
                parity = (parity_of_step - lag) % BUFS
                fn(s - lag, parity, pair - (lag + parity - parity_of_step) // BUFS)

    first = (deepest // BUFS + 1) * BUFS
    last = first + (count - 1 - first) // BUFS * BUFS
    for s in range(first):
        step(s, None, None)
    with eng.Fori(first // BUFS, last // BUFS) as pair:
        for u in range(BUFS):
            step(pair * BUFS + u, u, pair)
    for s in range(last, count + deepest):
        step(s, None, None)


class Core:
    pass


def wait_at_gate(eng, sem, value, gate):
    eng.wait_ge(sem, value)
    eng.sem_inc(gate, 1)


def new_semaphores(nc, ctx, prefix, names):
    return [ctx.enter_context(nc.semaphore(f"{prefix}_{n}")) for n in names.split()]


def blocks_of(ap, n, width=D):
    return ap.rearrange("p (n d) -> p n d", d=width)


def bcast_mid(ap, n):
    return ap.unsqueeze(1).to_broadcast([ap.shape[0], n, ap.shape[1]])


def bcast_last(ap, n):
    return ap.unsqueeze(2).to_broadcast([ap.shape[0], ap.shape[1], n])


def build_embed(nc, m, x, txt, tok_wT, tok_b, cls, pos, attn_w, alpha, beta, wqT, bq, keysT):
    with ExitStack() as ctx:
        (sorted_, const_in, pos_in, row_in, weights_in, zeroed, ident_made, transposed, dve_copied, act_copied,
         chunk_done, acc_read, cls_made, stat_step, gate) = new_semaphores(
            nc, ctx, "e", "sorted const_in pos_in row_in weights_in zeroed ident_made transposed "
            "dve_copied act_copied chunk_done acc_read cls_made stat_step gate")
        X_CREDIT = 2 * X_RING
        x_in = [ctx.enter_context(nc.semaphore(f"e_x_in{i}")) for i in range(X_RING)]

        o = 0
        xbuf = m.work[:, o:o + X_RING * ROWS * IMG].rearrange("p (s r w) -> p s r w", s=X_RING, w=IMG)
        o += X_RING * ROWS * IMG
        xsort = m.work[:, o:o + X_RING * ROWS * IMG].rearrange("p (s g k) -> p s g k", s=X_RING, g=GRID)
        o += X_RING * ROWS * IMG
        xT = m.work[:, o:o + T_RING * GRID * P].rearrange("p (s g b) -> p s g b", s=T_RING, b=P)
        o += T_RING * GRID * P
        posb = m.work[:, o:o + N_IMG_TOK * D].rearrange("p (n d) -> p n d", d=D)
        wT = m.scratch[0:KC, 0:CHUNKS * D].rearrange("p (k d) -> p k d", d=D)
        o = CHUNKS * D
        ones = m.scratch[0:1, o:o + P]
        bias4 = m.scratch[0:1, o + P:o + P + BANK]
        clsb = m.scratch[:, o + P + BANK:o + P + BANK + D]
        acc = m.ps[:, 0:2, :]
        tp = m.ps[0:KC, 2:2 + 2 * T_RING, :]
        x_v = x.rearrange("b c (g s r) w -> b c g s (r w)", g=GRID, r=ROWS)
        pos_v = pos.rearrange("n d -> (n d)").partition_broadcast(P).rearrange("p (n d) -> p n d", d=D)
        N_CONST, N_POS_IN = 16 * 5, 16 * 2
        N_WEIGHTS = 16 * (5 + len(attn_w) + 2)

        block = ctx.enter_context(nc.Block())

        @block.sync
        def _(sp):
            with sp.Fori(0, GRID) as gy:
                for k in range(CHUNKS):
                    sp.wait_ge(sorted_, gy * CHUNKS + (k + 1))
                    sp.dma_start(xbuf[:, k % X_RING].rearrange("p r w -> p (r w)"),
                                 x_v[:, k // STRIPS, gy, k % STRIPS, :]).then_inc(x_in[k % X_RING], 16)

        @block.scalar
        def _(act):
            for r in range(4):
                act.dma_start(bias4[:, r * D:(r + 1) * D], tok_b.rearrange("(a d) -> a d", a=1)).then_inc(const_in, 16)
            act.dma_start(wT, tok_wT).then_inc(const_in, 16)
            act.wait_ge(x_in[X_RING - 1], 16)
            act.dma_start(posb[:, 0, :], pos[0, :].partition_broadcast(P)).then_inc(pos_in, 16)
            act.dma_start(clsb, cls.rearrange("a d -> (a d)").partition_broadcast(P)).then_inc(pos_in, 16)
            act.dma_start(m.h[:, N_POS - TXT_REST:N_POS, :], txt[:, N_TXT - TXT_REST:N_TXT, :]).then_inc(weights_in, 16)
            for n, w in enumerate(attn_w):
                act.dma_start(m.attn_w[:, n, :], w).then_inc(weights_in, 16)
            act.dma_start(m.alphab[:, :], alpha.partition_broadcast(P)).then_inc(weights_in, 16)
            act.dma_start(m.betab[:, :], beta.partition_broadcast(P)).then_inc(weights_in, 16)
            act.dma_start(m.wqT[:, :], wqT).then_inc(weights_in, 16)
            act.dma_start(m.bq[:, :], bq).then_inc(weights_in, 16)
            act.wait_ge(zeroed, 1)
            for half in range(2):
                act.dma_start(m.keys[64 * half:64 * half + 64, :, EXP * half:EXP * half + EXP],
                              keysT[64 * half:64 * half + 64]).then_inc(weights_in, 16)
            act.sem_inc(act_copied, T_RING)
            with act.Fori(0, GRID) as gy:
                act.dma_start(posb[:, bass.ds(gy * GRID + 1, GRID), :],
                              pos_v[:, bass.ds(gy * GRID + 1, GRID), :]).then_inc(row_in, 16)
                act.dma_start(m.h[:, bass.ds(gy * TXT_ROW + N_IMG_TOK, TXT_ROW), :],
                              txt[:, bass.ds(gy * TXT_ROW, TXT_ROW), :]).then_inc(row_in, 16)
                for k in range(CHUNKS):
                    n = gy * CHUNKS + k
                    act.wait_ge(transposed, n * 2 + (X_CREDIT + 2))
                    act.wait_ge(chunk_done, n + 1)
                    nc.scalar.activation(xT[0:KC, k % T_RING, HALF:GRID, :],
                                         blocks_of(tp[:, 2 * (k % T_RING) + 1, :], HALF), ACT.Copy).then_inc(act_copied, 1)
            act.wait_ge(weights_in, N_WEIGHTS)

        @block.gpsimd
        def _(pool):
            pool.memset(m.keys[:, :, :], 0.0).then_inc(zeroed, 1)
            pool.memset(m.ident[:, :], 0.0).then_inc(zeroed, 1)
            pool.wait_ge(zeroed, 2)
            pool.affine_select(out=m.ident[:, :], in_=m.ident[:, :], compare_op=ALU.not_equal, fill=1.0,
                               base=0, pattern=[[-1, P]], channel_multiplier=1).then_inc(ident_made, 1)
            pool.memset(ones, 1.0).then_inc(ident_made, 1)
            pool.iota(m.count[:, :], pattern=[[1, EXP]], base=0, channel_multiplier=0,
                      allow_small_or_imprecise_dtypes=True)

        @block.tensor
        def _(pe):
            pe.sem_inc(transposed, X_CREDIT)
            pe.sem_inc(chunk_done, T_RING)
            pe.wait_ge(ident_made, 2)
            pe.wait_ge(const_in, N_CONST)

            def transposes(gy, k, half):
                n = gy * CHUNKS + k
                pe.wait_ge([dve_copied, act_copied][half], n + 1)
                for g in range(HALF):
                    gx = HALF * half + g
                    last = pe.transpose(tp[:, 2 * (k % T_RING) + half, g * P:(g + 1) * P],
                                        xsort[:, k % X_RING, gx, :], m.ident[:, :])
                last.then_inc(transposed, 1)

            def products(gy, k):
                n = gy * CHUNKS + k
                pe.wait_ge(dve_copied, n + 1 + T_RING)
                pe.wait_ge(act_copied, n + 1 + T_RING)
                for g in range(GRID):
                    last = pe.matmul(acc[:, g // HALF, (g % HALF) * D:(g % HALF + 1) * D],
                                     xT[0:KC, k % T_RING, g, :], wT[:, k, :], start=False,
                                     stop=(k == CHUNKS - 1 and g % HALF == HALF - 1), skip_group_check=True)
                last.then_inc(chunk_done, 1)

            with pe.Fori(0, GRID) as gy:
                pe.wait_ge(acc_read, gy + 1)
                for b in range(2):
                    pe.matmul(acc[:, b, :], ones, bias4, start=True, stop=False, skip_group_check=True)
                for k in range(CHUNKS):
                    pe.wait_ge(sorted_, gy * CHUNKS + (k + 1 + X_RING))
                    transposes(gy, k, 0)
                    transposes(gy, k, 1)
                    if k >= PRODUCT_LAG:
                        products(gy, k - PRODUCT_LAG)
                for k in range(CHUNKS - PRODUCT_LAG, CHUNKS):
                    products(gy, k)

        @block.vector
        def _(dve):
            dve.sem_inc(sorted_, X_RING)
            dve.sem_inc(dve_copied, T_RING)
            dve.sem_inc(acc_read, 1)

            def sort(gy, k):
                n = gy * CHUNKS + k
                dve.wait_ge(x_in[k % X_RING], (gy * (CHUNKS // X_RING) + (k // X_RING + 1)) * 16)
                dve.wait_ge(transposed, n * 2 + 2)
                dve.tensor_copy(xsort[:, k % X_RING].rearrange("p g (r w) -> p g r w", w=PATCH),
                                xbuf[:, k % X_RING].rearrange("p r (g w) -> p g r w", w=PATCH)).then_inc(sorted_, 1)

            def text_statistics(gy, i):
                at = gy * TXT_ROW + (N_IMG_TOK + i * TXT_PIECE)
                group_statistics(dve, m, [(at, TXT_PIECE)], stat_step, (gy * (TXT_PIECES + 1) + i) * 3, gate)

            with dve.Fori(0, GRID) as gy:
                for k in range(SORT_AHEAD):
                    sort(gy, k)
                for k in range(CHUNKS):
                    n = gy * CHUNKS + k
                    if k + SORT_AHEAD < CHUNKS:
                        sort(gy, k + SORT_AHEAD)
                    dve.wait_ge(transposed, n * 2 + (X_CREDIT + 1))
                    dve.wait_ge(chunk_done, n + 1)
                    dve.tensor_copy(xT[0:KC, k % T_RING, 0:HALF, :],
                                    blocks_of(tp[:, 2 * (k % T_RING), :], HALF)).then_inc(dve_copied, 1)
                    if k in TXT_AT:
                        if k == TXT_AT[0]:
                            dve.wait_ge(row_in, gy * 32 + 32)
                        text_statistics(gy, TXT_AT.index(k))
                dve.wait_ge(chunk_done, gy * CHUNKS + CHUNKS + T_RING)
                for b in range(2):
                    at = gy * GRID + (1 + HALF * b)
                    last = dve.tensor_tensor(m.h[:, bass.ds(at, HALF), :], blocks_of(acc[:, b, :], HALF),
                                             posb[:, bass.ds(at, HALF), :], ALU.mult)
                last.then_inc(acc_read, 1)
                dve.wait_ge(acc_read, gy + 2)
                group_statistics(dve, m, [(gy * GRID + 1, GRID)], stat_step, (gy * (TXT_PIECES + 1) + TXT_PIECES) * 3, gate)
            dve.wait_ge(pos_in, N_POS_IN)
            dve.tensor_tensor(m.h[:, 0, :], clsb, posb[:, 0, :], ALU.mult).then_inc(cls_made, 1)


def reciprocal_deviations(nc, dve, act, m, step, root_done, variances_ready):
    var, t = m.stat[:, :, 1], m.newton
    if act is not None:
        act.wait_ge(step, variances_ready + 1)
        nc.scalar.activation(m.rstd[:, :], t[:, :], ACT.Sqrt).then_inc(root_done, 1)
        return
    dve.wait_ge(step, variances_ready)
    dve.tensor_scalar(t[:, :], var, EPS, None, ALU.add).then_inc(step, 1)
    dve.wait_ge(root_done, 1)
    dve.reciprocal(m.rstd[:, :], m.rstd[:, :]).then_inc(step, 1)
    dve.wait_ge(step, variances_ready + 2)
    dve.tensor_tensor(t[:, :], t[:, :], m.rstd[:, :], ALU.mult).then_inc(step, 1)
    dve.wait_ge(step, variances_ready + 3)
    dve.tensor_tensor(t[:, :], t[:, :], m.rstd[:, :], ALU.mult).then_inc(step, 1)
    dve.wait_ge(step, variances_ready + 4)
    dve.tensor_scalar(t[:, :], t[:, :], -0.5, 1.5, ALU.mult, ALU.add).then_inc(step, 1)
    dve.wait_ge(step, variances_ready + 5)
    dve.tensor_tensor(m.rstd[:, :], m.rstd[:, :], t[:, :], ALU.mult).then_inc(step, 1)
    dve.wait_ge(step, variances_ready + 6)


def group_statistics(dve, m, groups, step, before, gate):
    dve.sem_inc(gate, 1)
    positions = [at + j for at, n in groups for j in range(n)]
    for i, position in enumerate(positions):
        last = dve.bn_stats(m.bn6[:, i, :], m.h[:, position, :])
    last.then_inc(step, 1)
    wait_at_gate(dve, step, before + 1, gate)
    for i in range(len(positions)):
        last = dve.bn_aggr(m.bn2[:, i, :], m.bn6[:, i, :])
    last.then_inc(step, 1)
    dve.wait_ge(step, before + 2)
    i = 0
    for at, n in groups:
        last = dve.tensor_copy(m.stat[:, bass.ds(at, n), :], m.bn2[:, i:i + n, :])
        i += n
    last.then_inc(step, 1)


def build_statistics(nc, m):
    with ExitStack() as ctx:
        step, root_done, gate = new_semaphores(nc, ctx, "n", "step root_done gate")
        block = ctx.enter_context(nc.Block())

        @block.vector
        def _(dve):
            dve.tensor_scalar(m.alphab[:, :], m.alphab[:, :], SCALE, None, ALU.mult)
            dve.tensor_scalar(m.betab[:, :], m.betab[:, :], SCALE, None, ALU.mult)
            group_statistics(dve, m, [(0, 1), (N_POS - TXT_REST, TXT_REST)], step, 0, gate)
            reciprocal_deviations(nc, dve, None, m, step, root_done, 3)

        @block.scalar
        def _(act):
            reciprocal_deviations(nc, None, act, m, step, root_done, 3)


class Softmax:

    def __init__(self, m):
        o = 0

        def take(n):
            nonlocal o
            o += n
            return m.scratch[:, o - n:o]

        self.xn = [take(BANK) for _ in range(BUFS)]
        self.xT = [take(BANK) for _ in range(BUFS)]
        self.s = [take(BANK) for _ in range(BUFS)]
        self.e = [take(BANK) for _ in range(BUFS)]
        self.r = [take(BANK) for _ in range(BUFS)]
        self.w = [take(BANK) for _ in range(BUFS)]
        self.neg_max = [take(GRP) for _ in range(BUFS)]
        self.sum = [take(GRP) for _ in range(BUFS)]
        self.rec = [take(GRP) for _ in range(BUFS)]
        assert o <= m.small


def softmax_stages(nc, m, b, sems, r_bank, total):
    (logits, exped, weighed, divided, summed) = sems

    def exps(act):
        def fn(g, p, pair):
            act.wait_ge(logits, g + 1 + BUFS)
            act.wait_ge(weighed, g + 1)
            for j in range(group_size(g)):
                last = nc.scalar.activation(b.e[p][:, j * D:(j + 1) * D], b.s[p][:, j * D:(j + 1) * D], ACT.Exp,
                                            bias=b.neg_max[p][:, j:j + 1], accum_out=b.sum[p][:, j:j + 1])
            last.then_inc(exped, 1)
        return fn

    def divide(pool):
        def fn(g, p, pair):
            n = group_size(g)
            pool.wait_ge(weighed, g + 1 + BUFS)
            w = blocks_of(b.w[p][:, 0:n * D], n)
            pool.tensor_tensor(w, w, bcast_last(b.rec[p][:, 0:n], D), ALU.mult).then_inc(divided, 1)
        return fn

    def sum_up(pe):
        def fn(g, p, pair):
            n = group_size(g)
            pe.wait_ge(divided, g + 1)
            pe.matmul(total[:, 0:n * D], m.ident[:, :], b.w[p][:, 0:n * D], start=isinstance(g, int) and g == 0,
                      stop=isinstance(g, int) and g == N_GRP - 1, skip_group_check=True).then_inc(summed, 1)
        return fn

    return exps, divide, sum_up


def build_query(nc, m):
    b = Softmax(m)
    with ExitStack() as ctx:
        (normed, norm_step, turned, copied, projected, logits, exped, weighed, divided, summed,
         step, done) = new_semaphores(nc, ctx, "q", "normed norm_step turned copied projected logits "
                                      "exped weighed divided summed step done")
        saved = [ctx.enter_context(nc.semaphore(f"q_saved{p}")) for p in range(BUFS)]
        turn = [m.ps[:, p, :] for p in range(BUFS)]
        q = [m.ps[:, BUFS + p, :] for p in range(BUFS)]
        total = m.ps[:, 2 * BUFS, :]
        exps, divide, sum_up = softmax_stages(nc, m, b, (logits, exped, weighed, divided, summed), q, total)
        block = ctx.enter_context(nc.Block())

        @block.gpsimd
        def _(pool):
            def norm(g, p, pair):
                n, at = group_size(g), g * GRP
                x = blocks_of(b.xn[p][:, 0:n * D], n)
                pool.wait_ge(turned, g + 1)
                pool.tensor_tensor(x, m.h[:, bass.ds(at, n), :],
                                   m.stat[:, bass.ds(at, n), 0:1].to_broadcast([P, n, D]), ALU.subtract).then_inc(norm_step, 1)
                pool.wait_ge(norm_step, g + 1)
                pool.tensor_tensor(x, x, m.rstd[:, bass.ds(at, n)].unsqueeze(2).to_broadcast([P, n, D]),
                                   ALU.mult).then_inc(normed, 1)

            run_skewed(pool, N_GRP, [(0, norm), (5, divide(pool))])

        @block.sync
        def _(sp):
            for p in range(BUFS):
                sp.sem_inc(saved[p], 16)

            def save(g, p, pair):
                n, at = group_size(g), g * GRP
                sp.wait_ge(copied, g + 1 + BUFS)
                sp.dma_start(m.work[:, bass.ds(at * D, n * D)], b.xT[p][:, 0:n * D]).then_inc(saved[p], 16)

            run_skewed(sp, N_GRP, [(0, save)])
            for p in range(BUFS):
                sp.wait_ge(saved[p], 16 * (1 + N_GRP // BUFS))

        @block.scalar
        def _(act):
            act.sem_inc(copied, BUFS)
            act.sem_inc(exped, BUFS)

            def copy(g, p, pair):
                n = group_size(g)
                act.wait_ge(turned, g + 1 + BUFS)
                act.wait_ge(projected, g + 1)
                act.wait_ge(saved[p], pair * 16 + 16)
                nc.scalar.activation(b.xT[p][:, 0:n * D], turn[p][:, 0:n * D], ACT.Copy).then_inc(copied, 1)

            run_skewed(act, N_GRP, [(0, copy), (1, exps(act))])

        @block.tensor
        def _(pe):
            pe.sem_inc(turned, BUFS)
            pe.sem_inc(projected, BUFS)
            pe.sem_inc(summed, BUFS)

            def turn_over(g, p, pair):
                pe.wait_ge(normed, g + 1)
                pe.wait_ge(copied, g + 1)
                for j in range(group_size(g)):
                    last = pe.transpose(turn[p][:, j * D:(j + 1) * D], b.xn[p][:, j * D:(j + 1) * D], m.ident[:, :])
                last.then_inc(turned, 1)

            def project(g, p, pair):
                pe.wait_ge(copied, g + 1 + BUFS)
                pe.wait_ge(weighed, g + 1)
                for j in range(group_size(g)):
                    last = pe.matmul(q[p][:, j * D:(j + 1) * D], b.xT[p][:, j * D:(j + 1) * D], m.attn_w[:, 0, :],
                                     start=True, stop=True)
                last.then_inc(projected, 1)

            run_skewed(pe, N_GRP, [(0, turn_over), (1, project), (5, sum_up(pe))])

        @block.vector
        def _(dve):
            dve.sem_inc(logits, BUFS)
            dve.sem_inc(weighed, BUFS)

            def logit(g, p, pair):
                n = group_size(g)
                s = blocks_of(b.s[p][:, 0:n * D], n)
                dve.wait_ge(projected, g + 1 + BUFS)
                dve.wait_ge(exped, g + 1)
                dve.tensor_tensor(s, blocks_of(q[p][:, 0:n * D], n), bcast_mid(m.alphab[:, :], n), ALU.mult).then_inc(step, 1)
                dve.wait_ge(step, g + 1)
                dve.tensor_reduce(b.neg_max[p][:, 0:n], s, AX.X, ALU.max, negate=True).then_inc(logits, 1)

            def weigh(g, p, pair):
                n = group_size(g)
                hg = m.h[:, bass.ds(g * GRP, n), :]
                q_g = blocks_of(q[p][:, 0:n * D], n)
                dve.wait_ge(exped, g + 1 + BUFS)
                dve.wait_ge(summed, g + 1)
                dve.reciprocal(b.rec[p][:, 0:n], b.sum[p][:, 0:n])
                dve.tensor_tensor(hg, hg, q_g, ALU.add)
                dve.tensor_tensor(b.w[p][:, 0:n * D], b.e[p][:, 0:n * D], q[p][:, 0:n * D], ALU.mult).then_inc(weighed, 1)

            run_skewed(dve, N_GRP, [(2, weigh), (0, logit)])
            dve.wait_ge(summed, N_GRP + BUFS)
            dve.tensor_reduce(m.gq[:, :], total.rearrange("p (n d) -> p d n", d=D), AX.X, ALU.add).then_inc(done, 1)


def build_key(nc, m):
    b = Softmax(m)
    with ExitStack() as ctx:
        (k_ready, r_ready, logits, exped, weighed, divided, summed, step, done) = new_semaphores(
            nc, ctx, "k", "k_ready r_ready logits exped weighed divided summed step done")
        loaded = [ctx.enter_context(nc.semaphore(f"k_loaded{p}")) for p in range(BUFS)]
        k = [m.ps[:, p, :] for p in range(BUFS)]
        total = m.ps[:, BUFS, :]
        exps, divide, sum_up = softmax_stages(nc, m, b, (logits, exped, weighed, divided, summed), k, total)
        block = ctx.enter_context(nc.Block())

        @block.sync
        def _(sp):
            def load(g, p, pair):
                n, at = group_size(g), g * GRP
                sp.wait_ge(k_ready, g + 1)
                sp.dma_start(b.xT[p][:, 0:n * D], m.work[:, bass.ds(at * D, n * D)]).then_inc(loaded[p], 16)

            run_skewed(sp, N_GRP, [(0, load)])

        @block.tensor
        def _(pe):
            pe.sem_inc(k_ready, BUFS)
            pe.sem_inc(summed, BUFS)

            def project(g, p, pair):
                pe.wait_ge(loaded[p], pair * 16 + 16)
                pe.wait_ge(r_ready, g + 1)
                for j in range(group_size(g)):
                    last = pe.matmul(k[p][:, j * D:(j + 1) * D], b.xT[p][:, j * D:(j + 1) * D], m.attn_w[:, 1, :],
                                     start=True, stop=True)
                last.then_inc(k_ready, 1)

            run_skewed(pe, N_GRP, [(0, project), (4, sum_up(pe))])

        @block.scalar
        def _(act):
            act.sem_inc(exped, BUFS)
            run_skewed(act, N_GRP, [(0, exps(act))])

        @block.gpsimd
        def _(pool):
            run_skewed(pool, N_GRP, [(0, divide(pool))])

        @block.vector
        def _(dve):
            dve.sem_inc(r_ready, BUFS)
            dve.sem_inc(logits, BUFS)
            dve.sem_inc(weighed, BUFS)

            def logit(g, p, pair):
                n = group_size(g)
                r, s = (blocks_of(x[p][:, 0:n * D], n) for x in (b.r, b.s))
                dve.wait_ge(k_ready, g + 1 + BUFS)
                dve.wait_ge(exped, g + 1)
                dve.wait_ge(weighed, g + 1)
                dve.tensor_tensor(r, blocks_of(k[p][:, 0:n * D], n), bcast_mid(m.gq[:, :], n), ALU.mult).then_inc(r_ready, 1)
                dve.wait_ge(r_ready, g + 1 + BUFS)
                dve.tensor_tensor(s, r, bcast_mid(m.betab[:, :], n), ALU.mult).then_inc(step, 1)
                dve.wait_ge(step, g + 1)
                dve.tensor_reduce(b.neg_max[p][:, 0:n], s, AX.X, ALU.max, negate=True).then_inc(logits, 1)

            def weigh(g, p, pair):
                n = group_size(g)
                dve.wait_ge(exped, g + 1 + BUFS)
                dve.wait_ge(summed, g + 1)
                dve.reciprocal(b.rec[p][:, 0:n], b.sum[p][:, 0:n])
                dve.tensor_tensor(b.w[p][:, 0:n * D], b.e[p][:, 0:n * D], b.r[p][:, 0:n * D], ALU.mult).then_inc(weighed, 1)

            run_skewed(dve, N_GRP, [(2, weigh), (0, logit)])
            dve.wait_ge(summed, N_GRP + BUFS)
            dve.tensor_reduce(m.gk[:, :], total.rearrange("p (n d) -> p d n", d=D), AX.X, ALU.add).then_inc(done, 1)


def build_value(nc, m, hmid):
    with ExitStack() as ctx:
        (stored, gate, gk_turned, gk_copied, v_ready, v_copied, kv_ready, o_ready, step, added, root_done) = new_semaphores(
            nc, ctx, "v", "stored gate gk_turned gk_copied v_ready v_copied kv_ready o_ready step added root_done")
        v = [m.ps[:, p, :] for p in range(BUFS)]
        out = [m.ps[:, BUFS + p, :] for p in range(BUFS)]
        gk_ps = m.ps[:, 2 * BUFS, 0:P]
        gkT = m.scratch[:, 0:P]
        kv = [m.scratch[:, P + p * BANK:P + (p + 1) * BANK] for p in range(BUFS)]
        v_sb = [m.scratch[:, P + p * BANK:P + (p + 1) * BANK] for p in range(BUFS, 2 * BUFS)]
        block = ctx.enter_context(nc.Block())

        @block.sync
        def _(sp):
            def store(g, p, pair):
                n, at = group_size(g), g * GRP
                sp.wait_ge(added, g + 1 + BUFS)
                sp.dma_start(hmid[:, bass.ds(at, n), :], m.h[:, bass.ds(at, n), :]).then_inc(stored, 16)

            run_skewed(sp, N_GRP, [(0, store)])
            sp.wait_ge(stored, 16 * N_GRP)

        @block.tensor
        def _(pe):
            pe.sem_inc(v_ready, BUFS)
            pe.sem_inc(o_ready, BUFS)
            pe.transpose(gk_ps, m.gk[:, :], m.ident[:, :]).then_inc(gk_turned, 1)

            def value(g, p, pair):
                n, at = group_size(g), g * GRP
                pe.wait_ge(v_copied, g + 1)
                pe.matmul(v[p][:, 0:n * D], m.attn_w[:, 2, :], m.work[:, bass.ds(at * D, n * D)],
                          start=True, stop=True).then_inc(v_ready, 1)

            def out_project(g, p, pair):
                pe.wait_ge(kv_ready, g + 1 + BUFS)
                pe.wait_ge(added, g + 1)
                for j in range(group_size(g)):
                    last = pe.matmul(out[p][:, j * D:(j + 1) * D], kv[p][:, j * D:(j + 1) * D], m.attn_w[:, 3, :],
                                     start=True, stop=True)
                last.then_inc(o_ready, 1)

            run_skewed(pe, N_GRP, [(0, value), (2, out_project)])

        @block.vector
        def _(dve):
            dve.sem_inc(added, BUFS)
            dve.wait_ge(gk_turned, 1)
            dve.tensor_copy(gkT, gk_ps).then_inc(gk_copied, 1)

            def add(g, p, pair):
                n = group_size(g)
                hg = m.h[:, bass.ds(g * GRP, n), :]
                dve.wait_ge(o_ready, g + 1 + BUFS)
                dve.tensor_tensor(hg, hg, blocks_of(out[p][:, 0:n * D], n), ALU.add).then_inc(added, 1)
                dve.wait_ge(added, g + 1 + BUFS)
                group_statistics(dve, m, [(g * GRP, n)], step, g * 3, gate)

            run_skewed(dve, N_GRP, [(0, add)])
            reciprocal_deviations(nc, dve, None, m, step, root_done, 3 * N_GRP)

        @block.gpsimd
        def _(pool):
            pool.sem_inc(kv_ready, BUFS)
            pool.wait_ge(gk_copied, 1)

            def times_key(g, p, pair):
                n = group_size(g)
                pool.wait_ge(v_copied, g + 1 + BUFS)
                pool.wait_ge(o_ready, g + 1)
                pool.tensor_tensor(blocks_of(kv[p][:, 0:n * D], n), blocks_of(v_sb[p][:, 0:n * D], n),
                                   bcast_mid(gkT, n), ALU.mult).then_inc(kv_ready, 1)

            run_skewed(pool, N_GRP, [(0, times_key)])

        @block.scalar
        def _(act):
            act.sem_inc(v_copied, BUFS)

            def copy(g, p, pair):
                n = group_size(g)
                act.wait_ge(v_ready, g + 1 + BUFS)
                act.wait_ge(kv_ready, g + 1)
                nc.scalar.activation(v_sb[p][:, 0:n * D], v[p][:, 0:n * D], ACT.Copy).then_inc(v_copied, 1)

            run_skewed(act, N_GRP, [(0, copy)])
            reciprocal_deviations(nc, None, act, m, step, root_done, 3 * N_GRP)


GATHERED = 3
ROUND_POS = GATHERED + 1
ROUNDS = N_POS // ROUND_POS
TAIL_POS = N_POS - ROUNDS * ROUND_POS
STEPS = GATHERED * HEADS

NORM, SECOND_HALF, TOP_A, TOP_B, PAIRS_PHASE, INDEX = range(6)
PREP_AT, DENSE_PREP_AT, SPLIT_AT = 5, 0, 6
HALF_HEADS = HEADS // 2
SPLIT_STEP = (GATHERED - 1) * HEADS + SPLIT_AT

CHUNK_BLOCKS = 8
BANK_BLOCKS = BANK // P
CHUNK_RING = 4
TABLE_CHUNKS = EXP // CHUNK_BLOCKS
ROUND_CHUNKS = 2 * TABLE_CHUNKS
S_BANKS = EXP // BANK_BLOCKS
HOT = 4
ITEMS = P // (2 * HOT)
DOWN_AT = {0: 3, 1: 2, 2: 3, 3: 3, 4: 3, 5: 2}
UP_AT = {17: 2, 18: 2, 19: 3, 20: 3, 21: 2, 22: 2, 23: 2}
LAY_AT = [12, 14, 16, 17, 18, 20, 21, 22, 23, 24, 25, 26, 28, 29, 30, 32]
MAKE_AT = [9, 11] + LAY_AT[:-2]
SCALE_AT = [11] + LAY_AT[:-1]
WEIGH_AT = LAY_AT[1:] + [33]
HOT_BUFS = 3


def items_at(places, w, half_step):
    return [c for c, p in enumerate(places) if w.dense and p == half_step]


def share(table, at):
    before = sum(n for s, n in table.items() if s < at)
    return list(range(before, before + table.get(at, 0)))


assert sum(DOWN_AT.values()) == sum(UP_AT.values()) == TABLE_CHUNKS and len(LAY_AT) == ITEMS


class Window:

    def __init__(self, r, buf, dense=True, first=False, last=False):
        self.r, self.buf, self.dense, self.first = r, buf, dense, first
        self.tile = r * GATHERED + buf
        self.pos = r * ROUND_POS + buf
        self.last = last

    def target(self, ahead):
        buf = (self.buf + ahead) % GATHERED
        r = self.r + (self.buf + ahead) // GATHERED
        return r * ROUND_POS + buf, buf, r

    def preparations(self, head):
        found = []
        if head < PREP_AT:
            phase, q, ahead = head + HEADS - PREP_AT, self.r * ROUND_POS + (2 + self.buf), 1
            if not self.dense:
                q -= 1
        else:
            phase, q, ahead = head - PREP_AT, self.r * ROUND_POS + (3 + self.buf), 2
            if self.buf == GATHERED - 1 and not self.last:
                q += 1
        if phase <= INDEX and (self.dense or self.buf + ahead < TAIL_POS):
            found.append((q, phase, False) + self.target(ahead))
        if self.dense and not self.last and self.buf == GATHERED - 1 and DENSE_PREP_AT <= head < DENSE_PREP_AT + INDEX:
            found.append((self.r * ROUND_POS + (ROUND_POS + 1), head - DENSE_PREP_AT, True,
                          self.r * ROUND_POS + (ROUND_POS + GATHERED), GATHERED, None))
        return found


def earlier(w, head, lag):
    if w.first and w.buf == 0 and head < lag:
        return None
    return w.tile - int(head < lag), (w.buf - int(head < lag)) % GATHERED, (head - lag) % HEADS, w.tile * HEADS + (head - lag)

def last_step(lag):
    tile = ROUNDS * GATHERED + TAIL_POS - 1
    return tile, TAIL_POS - 1, HEADS - 1 - lag, tile * HEADS + HEADS - 1 - lag


def windows(eng, run):
    for buf in range(GATHERED):
        run(Window(0, buf, first=True))
    with eng.Fori(1, ROUNDS - 1) as r:
        for buf in range(GATHERED):
            run(Window(r, buf))
    for buf in range(GATHERED):
        run(Window(ROUNDS - 1, buf, last=True))
    for buf in range(TAIL_POS):
        run(Window(ROUNDS, buf, dense=False))


def build_experts(nc, m, table, down_t, up_t, hmid, out):
    with ExitStack() as ctx:
        (xn_made, x_turned, x_copied, q_made, q_biased, scored, keys_step, picked, weight_in,
         weights_exped, found) = new_semaphores(
            nc, ctx, "p", "xn_made x_turned x_copied q_made q_biased scored keys_step picked weight_in "
            "weights_exped found")
        (dots, gelu_in, tanhed, valued, diag_made, rows_used, gathering, sum_read, dve_gate) = new_semaphores(
            nc, ctx, "g", "dots gelu_in tanhed valued diag_made rows_used gathering sum_read dve_gate")
        rows_in = [ctx.enter_context(nc.semaphore(f"g_rows_in{h}")) for h in range(HEADS)]
        (split_step, split_made, split_turned, coef_made, hot_made, hot_scaled, g_made, v_done, s_made,
         s_taken, up_used, dense_read) = new_semaphores(
            nc, ctx, "d", "split_step split_made split_turned coef_made hot_made hot_scaled g_made v_done s_made "
            "s_taken up_used dense_read")
        chunk_in = [ctx.enter_context(nc.semaphore(f"d_chunk_in{i}")) for i in range(CHUNK_RING)]
        h_in = [ctx.enter_context(nc.semaphore(f"h_in{b}")) for b in range(GATHERED)]
        h_stored = [ctx.enter_context(nc.semaphore(f"h_stored{b}")) for b in range(GATHERED)]
        dense_in, dense_res_in, dense_stored = new_semaphores(nc, ctx, "h", "dense_in dense_res_in dense_stored")

        n_rows, n_v, n_ring = HEADS * TOPK * ROW, EXP * P, CHUNK_RING * CHUNK_BLOCKS * P
        assert n_rows + n_v + n_ring <= BIG
        rows = m.big[:, 0:n_rows].rearrange("p (s r) -> p s r", r=ROW)
        v = m.big[:, n_rows:n_rows + n_v].rearrange("p (b t) -> p b t", t=P)
        ring = m.big[:, n_rows + n_v:n_rows + n_v + n_ring].rearrange(
            "p (c b k) -> p c b k", c=CHUNK_RING, b=CHUNK_BLOCKS)
        o = 0

        def take(n, dtype=F32):
            nonlocal o
            o += n
            assert o <= SCRATCH, o
            ap = m.scratch[:, o - n:o]
            return ap if dtype == F32 else ap.bitcast(dtype)

        xn = [take(D) for _ in range(GATHERED + 1)]
        xT = take(P)
        dense_xT = take(P)
        qT = take(HEADS * P)
        best = take(2 * HEADS * TOPK)
        best_no = take(2 * HEADS * TOPK, U32)
        cand = take(HEADS * N_CAND)
        cand_expert = take(HEADS * N_CAND)
        top = take(HEADS * TOPK)
        top_no = take(HEADS * TOPK, U32)
        hit = take(HEADS * TOPK * N_CAND)
        expert = take(HEADS * TOPK)
        experts = [take(HEADS * TOPK, U32) for _ in range(GATHERED + 1)]
        wexp = take(HEADS * TOPK)
        wsum = take(HEADS)
        weight = [take(HEADS * TOPK) for _ in range(GATHERED + 1)]
        h_buf = [take(D) for _ in range(GATHERED)]
        dot = take(HEADS * TOPK)
        square = take(TOPK)
        gin = take(2 * TOPK)
        th = take(2 * TOPK)
        half_xw = take(2 * TOPK)
        value = take(2 * TOPK)
        diag = take(2 * TOPK * P)
        dense_h = take(D)
        dense_res = take(D)
        e1_no = take(HEADS * TOPK, U32)
        e2_no = take(HEADS * TOPK, U32)
        split = take(3 * P).rearrange("p (c n k) -> p c n k", c=3, n=2)
        coef = take(3 * P // 2).rearrange("p (c t) -> p c t", c=3)
        hot1 = [take(HOT * EXP) for _ in range(HOT_BUFS)]
        hot2 = [take(HOT * EXP) for _ in range(HOT_BUFS)]

        x_ps = m.ps[:, 0, 0:P]
        split_ps = m.ps[:, 0, P:4 * P].rearrange("p (c t) -> p c t", c=3)
        q_ps = m.ps[:, 1, :].rearrange("p (h i) -> p h i", i=P)
        s_ps = m.ps[:, 2:4, :].rearrange("p b (h e) -> p (b h) e", e=EXP)
        up_ps = m.ps[:, 4, 0:D]
        dense_ps = m.ps[:, 5, 0:D]
        work_ps = [m.ps[:, b, :].rearrange("p (n k) -> p n k", k=P) for b in (6, 7, 5)]
        G_BANKS = 3
        S_CREDIT, ROWS_CREDIT, DIAG_CREDIT, V_CREDIT, SUM_CREDIT = 2, HEADS, 2, G_BANKS, 1
        KEYS_STEPS = 9

        block = ctx.enter_context(nc.Block())

        @block.sync
        def _(sp):
            def stream(r):
                for c in range(ROUND_CHUNKS):
                    src = down_t if c < TABLE_CHUNKS else up_t
                    at = c % TABLE_CHUNKS * CHUNK_BLOCKS * P
                    old = c - CHUNK_RING
                    if 0 <= old < TABLE_CHUNKS:
                        sp.wait_ge(s_made, r * S_BANKS + (old + 1) * (CHUNK_BLOCKS // BANK_BLOCKS))
                    else:
                        old = c if old < 0 else old - TABLE_CHUNKS + CHUNK_RING
                        sp.wait_ge(up_used, r * TABLE_CHUNKS + (old + 1))
                    sp.dma_start(ring[:, c % CHUNK_RING].rearrange("p b k -> p (b k)"),
                                 src[:, at:at + CHUNK_BLOCKS * P]).then_inc(chunk_in[c % CHUNK_RING], 16)

            with sp.Fori(0, ROUNDS) as r:
                stream(r)

        @block.gpsimd
        def _(pool):
            def gather(w):
                wait_at_gate(pool, found, w.tile + 1, gathering)
                for head in range(HEADS):
                    wait_at_gate(pool, rows_used, w.tile * HEADS + (head + 1), gathering)
                    for k in range(head * TOPK, (head + 1) * TOPK):
                        pool.indirect_dma_start(out=rows[:, k, :], out_offset=None, in_=table,
                                                in_offset=bass.IndirectOffsetOnAxis(
                                                    ap=experts[w.buf][:, k:k + 1], axis=0)).then_inc(rows_in[head], 16)

            windows(pool, gather)

        @block.scalar
        def _(act):
            def copy_turned(q, to):
                act.wait_ge(x_turned, q + 1)
                nc.scalar.activation(to, x_ps, ACT.Copy).then_inc(x_copied, 1)

            def bias_queries(q, half):
                act.wait_ge(q_made, q * 2 + (half + 1))
                act.wait_ge(scored, q * 2 + (half + 1))
                for i in range(HALF_HEADS):
                    head = half * HALF_HEADS + i
                    last = nc.scalar.activation(qT[:, head * P:(head + 1) * P], q_ps[:, i, :], ACT.Identity,
                                                bias=m.bq[:, head:head + 1])
                last.then_inc(q_biased, 1)

            def exp_weights(q):
                act.wait_ge(weight_in, q + 1)
                nc.scalar.activation(wexp, wexp, ACT.Exp).then_inc(weights_exped, 1)

            def prepare(q, phase):
                if phase in (NORM, SECOND_HALF):
                    bias_queries(q, phase - NORM)
                if phase == PAIRS_PHASE:
                    exp_weights(q)

            def load(b, pos):
                act.dma_start(h_buf[b], hmid[:, pos, :]).then_inc(h_in[b], 16)

            def store_and_load(w, head):
                b = (w.buf - 1) % GATHERED
                r = w.r if w.buf else w.r - 1
                if not (w.first and w.buf == 0):
                    if head == 2:
                        act.wait_ge(sum_read, w.tile + SUM_CREDIT)
                        act.dma_start(out[:, w.pos - 1 if w.buf else w.pos - 2, :], h_buf[b]).then_inc(h_stored[b], 16)
                    if head == 4 and w.dense and not (isinstance(r, int) and r == ROUNDS - 1 and b >= TAIL_POS):
                        act.wait_ge(h_stored[b], r * 16 + 16)
                        load(b, (r + 1) * ROUND_POS + b)
                if w.buf == 0 and head == 3 and not w.first:
                    act.wait_ge(dense_read, w.r + 1)
                    act.dma_start(out[:, w.pos - 1, :], dense_res).then_inc(dense_stored, 16)
                if w.buf == 0 and head == 6 and w.dense:
                    if not w.first:
                        act.wait_ge(dense_stored, w.r * 16)
                    act.dma_start(dense_res, hmid[:, w.pos + GATHERED, :]).then_inc(dense_res_in, 16)
                if w.buf == 1 and head == 4 and w.dense and not (isinstance(w.r, int) and w.r == ROUNDS - 1):
                    act.wait_ge(xn_made, w.r * ROUND_POS + 2)
                    act.dma_start(dense_h, hmid[:, w.pos + (ROUND_POS + GATHERED - 1), :]).then_inc(dense_in, 16)

            def take_scores(w, c):
                for b in range(c * CHUNK_BLOCKS // BANK_BLOCKS, (c + 1) * CHUNK_BLOCKS // BANK_BLOCKS):
                    act.wait_ge(s_made, w.r * S_BANKS + (b + 1))
                    nc.scalar.activation(v[:, b * BANK_BLOCKS:(b + 1) * BANK_BLOCKS, :], work_ps[b % 2][:, :, :],
                                         ACT.Gelu_apprx_tanh).then_inc(s_taken, 1)

            def scale_hot(w, c):
                act.wait_ge(hot_made, w.r * ITEMS + (c + 1))
                for i in range(HOT):
                    t = c * HOT + i
                    hot = hot2[c % HOT_BUFS][:, i * EXP:(i + 1) * EXP]
                    last = nc.scalar.activation(hot, hot, ACT.Copy, scale=coef[:, 2, t:t + 1])
                last.then_inc(hot_scaled, 1)

            def tanh(w, head):
                k = head % 2
                act.wait_ge(gelu_in, w.tile * HEADS + (head + 1))
                nc.scalar.activation(th[:, k * TOPK:(k + 1) * TOPK], gin[:, k * TOPK:(k + 1) * TOPK], ACT.Tanh,
                                     scale=GELU_C * GELU_K).then_inc(tanhed, 1)

            def diagonals(tile, b, head, s):
                k = head % 2
                act.wait_ge(valued, s + 1)
                act.wait_ge(rows_used, s + (ROWS_CREDIT - 1))
                for k8 in range(TOPK):
                    i = k * TOPK + k8
                    last = nc.scalar.activation(diag[:, i * P:(i + 1) * P], m.ident[:, :], ACT.Copy,
                                                scale=value[:, i:i + 1])
                last.then_inc(diag_made, 1)

            def run(w):
                for head in range(HEADS):
                    at = w.buf * HEADS + head
                    preparations = w.preparations(head)
                    for q, phase, is_dense, *_ in preparations:
                        if phase == NORM:
                            copy_turned(q, dense_xT if is_dense else xT)
                    down = share(DOWN_AT, at) if w.dense else []
                    for c in down[:1]:
                        take_scores(w, c)
                    for c in items_at(SCALE_AT, w, 2 * at):
                        scale_hot(w, c)
                    tanh(w, head)
                    if earlier(w, head, 1):
                        diagonals(*earlier(w, head, 1))
                    for c in down[1:]:
                        take_scores(w, c)
                    for c in items_at(SCALE_AT, w, 2 * at + 1):
                        scale_hot(w, c)
                    for q, phase, *_ in preparations:
                        prepare(q, phase)
                    store_and_load(w, head)

            act.sem_inc(diag_made, DIAG_CREDIT)
            act.sem_inc(s_taken, S_CREDIT)
            for b in range(GATHERED):
                load(b, b)
            act.dma_start(dense_h, hmid[:, GATHERED, :]).then_inc(dense_in, 16)
            for q, to in enumerate((xT, dense_xT, xT)):
                copy_turned(q, to)
                bias_queries(q, 0)
                bias_queries(q, 1)
                if q < 2:
                    exp_weights(q)
            windows(act, run)
            diagonals(*last_step(0))
            act.wait_ge(sum_read, ROUNDS * GATHERED + TAIL_POS + SUM_CREDIT)
            act.dma_start(out[:, N_POS - 1, :], h_buf[TAIL_POS - 1]).then_inc(h_stored[TAIL_POS - 1], 16)
            for b in range(GATHERED):
                act.wait_ge(h_stored[b], 16 * (ROUNDS + (1 if b < TAIL_POS else 0)))
            act.wait_ge(dense_stored, 16 * ROUNDS)

        @block.tensor
        def _(pe):
            pe.sem_inc(scored, 2)
            pe.sem_inc(rows_used, ROWS_CREDIT)
            pe.sem_inc(up_used, CHUNK_RING)

            def turn(q, b):
                pe.wait_ge(xn_made, q + 1)
                pe.transpose(x_ps, xn[b], m.ident[:, :]).then_inc(x_turned, 1)

            def query(q, half, xT_of):
                pe.wait_ge(x_copied, q + 1)
                pe.wait_ge(q_biased, q * 2 + half) if not (isinstance(q, int) and q * 2 + half == 0) else None
                for i in range(HALF_HEADS):
                    head = half * HALF_HEADS + i
                    last = pe.matmul(q_ps[:, i, :], m.wqT[:, head * P:(head + 1) * P], xT_of, start=True, stop=True)
                last.then_inc(q_made, 1)

            def score(q, half):
                pe.wait_ge(q_biased, q * 2 + (half + 1))
                pe.wait_ge(picked, q * 2 + (half + 1))
                for i in range(HALF_HEADS):
                    head = half * HALF_HEADS + i
                    last = pe.matmul(s_ps[:, 2 * i:2 * i + 2, :], qT[:, head * P:(head + 1) * P],
                                     m.keys[:, head, :], start=True, stop=True)
                last.then_inc(scored, 1)

            def turn_split(r):
                pe.wait_ge(split_made, r + 1)
                for i in range(3):
                    last = pe.transpose(split_ps[:, i, :], split[:, i].rearrange("p n k -> p (n k)"), m.ident[:, :])
                last.then_inc(split_turned, 1)

            def dense_down(w, c):
                pe.wait_ge(chunk_in[c % CHUNK_RING], w.r * (16 * ROUND_CHUNKS // CHUNK_RING) + 16 * (c // CHUNK_RING + 1))
                for b in range(CHUNK_BLOCKS):
                    bank, col = divmod(c * CHUNK_BLOCKS + b, BANK_BLOCKS)
                    if col == 0:
                        pe.wait_ge(s_taken, w.r * S_BANKS + (bank + 1))
                    last = pe.matmul(work_ps[bank % 2][:, col, :], ring[:, c % CHUNK_RING, b, :], dense_xT, start=True, stop=True)
                    if col == BANK_BLOCKS - 1:
                        last.then_inc(s_made, 1)

            def lay_out(w, c):
                pe.wait_ge(hot_scaled, w.r * ITEMS + (c + 1))
                if c == 0:
                    pe.wait_ge(s_taken, w.r * S_BANKS + (S_BANKS + S_CREDIT))
                for side in range(2):
                    part = slice(P // 2 * side, P // 2 * (side + 1))
                    n = 2 * c + side
                    pe.wait_ge(v_done, w.r * (2 * ITEMS) + (n + 1))
                    if n == G_BANKS - 1:
                        pe.wait_ge(dense_read, w.r + 1)
                    for i in range(HOT):
                        last = pe.matmul(work_ps[n % G_BANKS][:, i, :], hot1[c % HOT_BUFS][part, i * EXP:(i + 1) * EXP],
                                         hot2[c % HOT_BUFS][part, i * EXP:(i + 1) * EXP], start=True, stop=True)
                    last.then_inc(g_made, 1)

            def dense_up(w, c):
                if c == 0:
                    pe.wait_ge(v_done, w.r * (2 * ITEMS) + (2 * ITEMS + V_CREDIT))
                    pe.wait_ge(dense_read, w.r + 1)
                n = TABLE_CHUNKS + c
                pe.wait_ge(chunk_in[n % CHUNK_RING], w.r * (16 * ROUND_CHUNKS // CHUNK_RING) + 16 * (n // CHUNK_RING + 1))
                for b in range(CHUNK_BLOCKS):
                    block_no = c * CHUNK_BLOCKS + b
                    last = pe.matmul(dense_ps, v[:, block_no, :], ring[:, n % CHUNK_RING, b, :],
                                     start=(block_no == 0), stop=(block_no == EXP - 1), skip_group_check=True)
                last.then_inc(up_used, 1)

            def head_sum(tile, b, head, s):
                if head == 0:
                    pe.wait_ge(sum_read, tile + SUM_CREDIT)
                pe.wait_ge(diag_made, s + (1 + DIAG_CREDIT))
                for k in range(TOPK):
                    i = (head % 2) * TOPK + k
                    last = pe.matmul(up_ps, diag[:, i * P:(i + 1) * P], rows[:, head * TOPK + k, D:ROW],
                                     start=(head == 0 and k == 0), stop=(head == HEADS - 1 and k == TOPK - 1),
                                     skip_group_check=True)
                last.then_inc(rows_used, 1)

            def run(w):
                for head in range(HEADS):
                    at = w.buf * HEADS + head
                    preparations = w.preparations(head)
                    for q, phase, is_dense, _, b, _ in preparations:
                        if phase == NORM:
                            turn(q, b)
                        if phase == SECOND_HALF:
                            score(q, 0)
                            query(q, 1, dense_xT if is_dense else xT)
                    if w.dense and not w.last and at == SPLIT_STEP + 1:
                        turn_split(w.r + 1)
                    if w.dense:
                        for c in share(DOWN_AT, at)[:1]:
                            dense_down(w, c)
                        for c in items_at(LAY_AT, w, 2 * at):
                            lay_out(w, c)
                    if earlier(w, head, 2):
                        head_sum(*earlier(w, head, 2))
                    if w.dense:
                        for c in share(DOWN_AT, at)[1:]:
                            dense_down(w, c)
                        for c in items_at(LAY_AT, w, 2 * at + 1):
                            lay_out(w, c)
                        for c in share(UP_AT, at):
                            dense_up(w, c)
                    for q, phase, is_dense, *_ in preparations:
                        if phase == NORM:
                            query(q, 0, dense_xT if is_dense else xT)
                        if phase == TOP_A:
                            score(q, 1)

            for q, b, xt in ((0, 0, xT), (1, GATHERED, dense_xT), (2, 1, xT)):
                turn(q, b)
                query(q, 0, xt)
                score(q, 0)
                query(q, 1, xt)
                score(q, 1)
                if q == 1:
                    turn_split(0)
            windows(pe, run)
            head_sum(*last_step(1))
            head_sum(*last_step(0))

        @block.vector
        def _(dve):
            dve.sem_inc(picked, 1)
            dve.sem_inc(sum_read, SUM_CREDIT)
            dve.sem_inc(dense_read, 1)
            dve.sem_inc(v_done, V_CREDIT)

            def normalise(h, pos, b):
                dve.tensor_scalar(xn[b], h, m.stat[:, pos, 0:1], m.rstd[:, bass.ds(pos, 1)],
                                  ALU.subtract, ALU.mult).then_inc(xn_made, 1)

            def best_keys(q, half):
                wait_at_gate(dve, scored, q * 2 + (half + 3), dve_gate)
                at = half * HALF_HEADS * 2
                for i in range(2 * HALF_HEADS):
                    last = dve.max(best[:, (at + i) * TOPK:(at + i + 1) * TOPK], s_ps[:, i, :])
                last.then_inc(keys_step, 1)
                wait_at_gate(dve, keys_step, q * KEYS_STEPS + (half + 1), dve_gate)
                for i in range(2 * HALF_HEADS):
                    j = slice((at + i) * TOPK, (at + i + 1) * TOPK)
                    last = dve.max_index(best_no[:, j], best[:, j], s_ps[:, i, :])
                last.then_inc(picked, 1)

            def best_pairs(q):
                dve.wait_ge(picked, q * 2 + 3)
                sc = best.rearrange("p (h c r) -> p h c r", c=2, r=TOPK)
                no = best_no.rearrange("p (h c r) -> p h c r", c=2, r=TOPK)
                sums = cand.rearrange("p (h c) -> p h c", c=N_CAND)
                numbers = cand_expert.rearrange("p (h c) -> p h c", c=N_CAND)
                at = 0
                for i0, ni, nj in PAIRS:
                    for i in range(i0, i0 + ni) if nj > 1 else [i0]:
                        w = nj if nj > 1 else ni
                        shape = [P, HEADS, w]
                        rank = slice(i, i + 1) if nj > 1 else slice(i0, i0 + ni)
                        dve.tensor_tensor(sums[:, :, at:at + w], sc[:, :, 0, rank].to_broadcast(shape),
                                          sc[:, :, 1, 0:nj].to_broadcast(shape), ALU.add)
                        last = dve.scalar_tensor_tensor(
                            out=numbers[:, :, at:at + w], in0=no[:, :, 0, rank].to_broadcast(shape), scalar=float(EXP),
                            in1=no[:, :, 1, 0:nj].to_broadcast(shape), op0=ALU.mult, op1=ALU.add)
                        at += w
                last.then_inc(keys_step, 1)
                wait_at_gate(dve, keys_step, q * KEYS_STEPS + 3, dve_gate)
                for head in range(HEADS):
                    last = dve.max(top[:, head * TOPK:(head + 1) * TOPK], cand[:, head * N_CAND:(head + 1) * N_CAND])
                last.then_inc(keys_step, 1)
                wait_at_gate(dve, keys_step, q * KEYS_STEPS + 4, dve_gate)
                for head in range(HEADS):
                    dve.max_index(top_no[:, head * TOPK:(head + 1) * TOPK], top[:, head * TOPK:(head + 1) * TOPK],
                                  cand[:, head * N_CAND:(head + 1) * N_CAND])
                t = top.rearrange("p (h r) -> p h r", r=TOPK)
                dve.tensor_tensor(wexp.rearrange("p (h r) -> p h r", r=TOPK), t,
                                  t[:, :, 0:1].to_broadcast([P, HEADS, TOPK]), ALU.subtract).then_inc(weight_in, 1)

            def expert_numbers(q, b, signal):
                dve.wait_ge(weight_in, q + 1)
                hits = hit.rearrange("p (k c) -> p k c", c=N_CAND)
                dve.tensor_tensor(hits, bcast_last(top_no, N_CAND), bcast_mid(m.count[:, 0:N_CAND], HEADS * TOPK),
                                  ALU.is_equal).then_inc(keys_step, 1)
                dve.wait_ge(keys_step, q * KEYS_STEPS + 5)
                by_head = hit.rearrange("p (h k c) -> p h k c", h=HEADS, c=N_CAND)
                dve.tensor_tensor(by_head, by_head,
                                  cand_expert.rearrange("p (h c) -> p h c", c=N_CAND).unsqueeze(2)
                                  .to_broadcast([P, HEADS, TOPK, N_CAND]), ALU.mult).then_inc(keys_step, 1)
                dve.wait_ge(keys_step, q * KEYS_STEPS + 6)
                dve.tensor_reduce(expert, hits, AX.X, ALU.add).then_inc(keys_step, 1)
                dve.wait_ge(keys_step, q * KEYS_STEPS + 7)
                dve.tensor_copy(experts[b], expert).then_inc(signal, 1)
                dve.wait_ge(weights_exped, q + 1)
                w = wexp.rearrange("p (h r) -> p h r", r=TOPK)
                dve.tensor_reduce(wsum, w, AX.X, ALU.add).then_inc(keys_step, 1)
                dve.wait_ge(keys_step, q * KEYS_STEPS + 8)
                dve.reciprocal(wsum, wsum).then_inc(keys_step, 1)
                dve.wait_ge(keys_step, q * KEYS_STEPS + 9)
                return dve.tensor_tensor(weight[b].rearrange("p (h r) -> p h r", r=TOPK), w, bcast_last(wsum, TOPK), ALU.mult)

            def split_pairs(r, q):
                expert_numbers(q, GATHERED, split_step).then_inc(split_step, 1)
                dve.wait_ge(split_step, r * 3 + 2)
                number = experts[GATHERED]
                dve.tensor_scalar(e1_no, number, EXP.bit_length() - 1, None, ALU.logical_shift_right)
                dve.tensor_scalar(e2_no, number, EXP - 1, None, ALU.bitwise_and).then_inc(split_step, 1)
                dve.wait_ge(split_step, r * 3 + 3)
                dve.tensor_copy(split[:, 0], bcast_mid(e1_no, 2))
                dve.tensor_copy(split[:, 1], bcast_mid(e2_no, 2))
                dve.tensor_copy(split[:, 2], bcast_mid(weight[GATHERED], 2)).then_inc(split_made, 1)

            def take_coef(w):
                dve.wait_ge(split_turned, w.r + 1)
                for side in range(2):
                    part = slice(P // 2 * side, P // 2 * (side + 1))
                    last = dve.tensor_copy(coef[part], split_ps[part, :, P // 2 * side:P // 2 * (side + 1)])
                last.then_inc(coef_made, 1)

            def make_hot(w, c):
                if c == 0:
                    dve.wait_ge(coef_made, w.r + 1)
                c_buf = c % HOT_BUFS
                for hot, row in ((hot1, 0), (hot2, 1)):
                    last = dve.tensor_tensor(blocks_of(hot[c_buf], HOT), bcast_mid(m.count[:, :], HOT),
                                             bcast_last(coef[:, row, c * HOT:(c + 1) * HOT], EXP), ALU.is_equal)
                last.then_inc(hot_made, 1)

            def weigh_values(w, c):
                if c == 0:
                    dve.wait_ge(s_taken, w.r * S_BANKS + (S_BANKS + S_CREDIT))
                for side in range(2):
                    n = 2 * c + side
                    dve.wait_ge(g_made, w.r * (2 * ITEMS) + (n + 1))
                    t = P // 2 * side + c * HOT
                    values = v[:, :, t:t + HOT].rearrange("p b t -> p t b")
                    dve.tensor_tensor(values, values, work_ps[n % G_BANKS][:, 0:HOT, :], ALU.mult).then_inc(v_done, 1)

            def items(w, half_step):
                for c in items_at(WEIGH_AT, w, half_step):
                    weigh_values(w, c)
                for c in items_at(MAKE_AT, w, half_step):
                    make_hot(w, c)

            def down(w, head):
                x = dot[:, head * TOPK:(head + 1) * TOPK]
                pair = slice((head % 2) * TOPK, (head % 2 + 1) * TOPK)
                dve.wait_ge(rows_in[head], w.tile * (16 * TOPK) + 16 * TOPK)
                for k in range(TOPK):
                    row = rows[:, head * TOPK + k, 0:D]
                    last = dve.tensor_tensor_reduce(row, row, xn[w.buf], 1.0, 0.0, ALU.mult, ALU.add, x[:, k:k + 1])
                last.then_inc(dots, 1)
                dve.wait_ge(dots, w.tile * (2 * HEADS) + (2 * head + 1))
                dve.tensor_tensor(square, x, x, ALU.mult).then_inc(dots, 1)
                dve.scalar_tensor_tensor(out=half_xw[:, pair], in0=x, scalar=0.5,
                                         in1=weight[w.buf][:, head * TOPK:(head + 1) * TOPK], op0=ALU.mult, op1=ALU.mult)
                dve.wait_ge(dots, w.tile * (2 * HEADS) + (2 * head + 2))
                dve.scalar_tensor_tensor(out=gin[:, pair], in0=square, scalar=1.0 / GELU_K, in1=x,
                                         op0=ALU.add, op1=ALU.mult).then_inc(gelu_in, 1)

            def gelu(tile, b, head, s):
                pair = slice((head % 2) * TOPK, (head % 2 + 1) * TOPK)
                dve.wait_ge(tanhed, s + 1)
                dve.wait_ge(diag_made, s + 1)
                dve.scalar_tensor_tensor(out=value[:, pair], in0=th[:, pair], scalar=1.0, in1=half_xw[:, pair],
                                         op0=ALU.add, op1=ALU.mult).then_inc(valued, 1)

            def add_sum(tiles, b):
                dve.wait_ge(rows_used, tiles * HEADS + ROWS_CREDIT)
                dve.tensor_tensor(h_buf[b], h_buf[b], up_ps, ALU.add).then_inc(sum_read, 1)

            def add_dense(rounds):
                dve.wait_ge(dense_res_in, rounds * 16)
                dve.wait_ge(up_used, rounds * TABLE_CHUNKS + CHUNK_RING)
                dve.tensor_tensor(dense_res, dense_res, dense_ps, ALU.add).then_inc(dense_read, 1)

            def run(w):
                for head in range(HEADS):
                    at = w.buf * HEADS + head
                    preparations = w.preparations(head)
                    for q, phase, is_dense, pos, b, r in preparations:
                        if phase == NORM:
                            if is_dense:
                                dve.wait_ge(dense_in, w.r * 16 + 32)
                            else:
                                dve.wait_ge(h_in[b], r * 16 + 16)
                            normalise(dense_h if is_dense else h_buf[b], pos, b)
                    items(w, 2 * at)
                    down(w, head)
                    if earlier(w, head, 1):
                        gelu(*earlier(w, head, 1))
                    for q, phase, _, _, b, _ in preparations:
                        if phase in (TOP_A, TOP_B):
                            best_keys(q, phase - TOP_A)
                        if phase == PAIRS_PHASE:
                            best_pairs(q)
                        if phase == INDEX:
                            expert_numbers(q, b, found)
                    if w.dense and not w.last and at == SPLIT_STEP:
                        split_pairs(w.r + 1, w.r * ROUND_POS + (ROUND_POS + 1))
                    if w.dense and at == 0:
                        take_coef(w)
                    items(w, 2 * at + 1)
                    if not (w.first and w.buf == 0):
                        if head == 1:
                            add_sum(w.tile, (w.buf - 1) % GATHERED)
                        if head == 1 and w.buf == 0:
                            add_dense(w.r)

            dve.wait_ge(h_in[0], 16)
            normalise(h_buf[0], 0, 0)
            best_keys(0, 0)
            best_keys(0, 1)
            best_pairs(0)
            expert_numbers(0, 0, found)
            dve.wait_ge(dense_in, 16)
            normalise(dense_h, GATHERED, GATHERED)
            best_keys(1, 0)
            best_keys(1, 1)
            best_pairs(1)
            split_pairs(0, 1)
            dve.wait_ge(h_in[1], 16)
            normalise(h_buf[1], 1, 1)
            best_keys(2, 0)
            windows(dve, run)
            gelu(*last_step(0))
            add_sum(ROUNDS * GATHERED + TAIL_POS, TAIL_POS - 1)


BIG = 36864
SCRATCH = 11600


def build(nc, x, txt, tok_wT, tok_b, cls, pos, wq, wk, wv, wr, alpha, beta, ffn_wqT, ffn_bq, keysT, table,
          down_t, up_t, out):
    hmid = nc.dram_tensor("hmid", (P, N_POS, D), F32, kind="Internal").ap()
    m = Core()
    with ExitStack() as ctx:
        def sb(name, shape):
            return ctx.enter_context(nc.sbuf_tensor(name, shape, F32))

        m.big = sb("big", [P, BIG])
        m.scratch = sb("scratch", [P, SCRATCH])
        m.h = m.big[:, 0:N_POS * D].rearrange("p (n d) -> p n d", d=D)
        m.work = m.big[:, N_POS * D:2 * N_POS * D]
        top = SCRATCH

        def keep(n):
            nonlocal top
            top -= n
            return m.scratch[:, top:top + n]

        m.attn_w = keep(4 * D).rearrange("p (n d) -> p n d", d=D)
        m.alphab, m.betab, m.gq, m.gk = (keep(D) for _ in range(4))
        m.newton = keep(N_POS)
        m.bn6 = keep(GRID * 6).rearrange("p (n k) -> p n k", k=6)
        m.bn2 = keep(GRID * 2).rearrange("p (n k) -> p n k", k=2)
        m.small = top
        m.ident = sb("ident", [P, P])
        m.wqT = sb("wqT", [P, HEADS * P])
        m.bq = sb("bq", [P, HEADS])
        m.keys = sb("keys", [P, HEADS, 2 * EXP])
        m.count = sb("count", [P, EXP])
        m.stat = sb("stat", [P, N_POS, 2])
        m.rstd = sb("rstd", [P, N_POS])
        m.ps = ctx.enter_context(nc.psum_tensor("ps", [P, 8, BANK], F32))
        build_embed(nc, m, x, txt, tok_wT, tok_b, cls, pos, [wq, wk, wv, wr], alpha, beta, ffn_wqT, ffn_bq, keysT)
        build_statistics(nc, m)
        build_query(nc, m)
        build_key(nc, m)
        build_value(nc, m, hmid)
        build_experts(nc, m, table, down_t, up_t, hmid, out)


def kernel(**inputs):
    import numpy as np
    from concourse import bacc
    from concourse.bass_utils import run_bass_kernel_spmd

    a = {k: np.asarray(v) for k, v in inputs.items()}
    down, up = a["L0_ffn_w_down_embed"], a["L0_ffn_w_up_embed"]
    data = {
        "x": a["x"], "txt": a["txt"],
        "tok_wT": a["L0_tok_W"].reshape(D, CHUNKS, KC).transpose(2, 1, 0),
        "tok_b": a["L0_tok_b"], "cls": a["L0_tok_class_token"], "pos": a["L0_tok_pos_embed"],
        "wq": a["L0_attn_Wq"], "wk": a["L0_attn_Wk"], "wv": a["L0_attn_Wv"], "wr": a["L0_attn_Wr"],
        "alpha": a["L0_attn_alpha"], "beta": a["L0_attn_beta"],
        "ffn_wqT": a["L0_ffn_Wq"].T,
        "ffn_bq": a["L0_ffn_bq"].reshape(HEADS, P).T,
        "keysT": a["L0_ffn_keys"].transpose(1, 3, 0, 2).reshape(P, HEADS, EXP),
        "table": np.concatenate([down, up], axis=1),
        "down_t": down.reshape(EXP, EXP, D).transpose(2, 1, 0).reshape(D, EXP * EXP),
        "up_t": up.reshape(EXP, EXP * D),
    }
    data = {k: np.ascontiguousarray(v) for k, v in data.items()}
    nc = bacc.Bacc("TRN2", target_bir_lowering=False, num_devices=1)
    aps = {k: nc.dram_tensor(f"in_{k}", v.shape, mybir.dt.from_np(v.dtype), kind="ExternalInput").ap()
           for k, v in data.items()}
    out = nc.dram_tensor("out_h", (P, N_POS, D), F32, kind="ExternalOutput").ap()
    build(nc, *aps.values(), out)
    r = run_bass_kernel_spmd(nc, [{f"in_{k}": v for k, v in data.items()}], core_ids=[0])
    return r.results[0]["out_h"]
```
